# Optimizing a Trainium2 kernel written in Bass

```python
import numpy as np
import jax
import jax.numpy as jnp

def _softmax(x, axis=-1):
    return jax.nn.softmax(x, axis=axis)

def _gelu(x):
    return jax.nn.gelu(x, approximate=True)

def _silu(x):
    return jax.nn.silu(x)

def _sigmoid(x):
    return jax.nn.sigmoid(x)

def _layernorm(x, axis=-1, eps=1e-05):
    m = jnp.mean(x, axis=axis, keepdims=True)
    v = jnp.var(x, axis=axis, keepdims=True)
    return (x - m) / jnp.sqrt(v + eps)

def _scatter_add(tgt, idx, src, axis=0):
    return tgt.at[idx].add(src)

def _segment_sum(src, seg, n):
    return jax.ops.segment_sum(src, seg, n)
kernel_name = 'mk_gnn_resnorm_d2_gnn_r32_90d917'

def setup_inputs(seed: int=0):
    np.random.seed(seed)
    _w = jnp.asarray

    def _rec_inputs():
        import jax
        import jax.numpy as jnp
        _gk = jax.random.key(seed)
        x = -0.0009044 + 1 * jax.random.normal(jax.random.fold_in(_gk, 1), (3125, 16), jnp.float32)
        _s = jax.random.randint(jax.random.fold_in(_gk, 2), (50000,), 0, 3125, jnp.int32)
        _d = jax.random.randint(jax.random.fold_in(_gk, 3), (50000,), 0, 3125, jnp.int32)
        _loop = jnp.arange(3125, dtype=jnp.int32)
        src = jnp.concatenate([_s, _d, _loop])
        dst = jnp.concatenate([_d, _s, _loop])
        _o = jnp.argsort(dst, stable=True)
        src = src[_o]
        dst = dst[_o]
        edge_attr_16 = -3.57403e-05 + 0.999761 * jax.random.normal(jax.random.fold_in(_gk, 12), (103125, 16), jnp.float32)
        return (x, src, dst, edge_attr_16)
    x, src, dst, edge_attr_16 = _rec_inputs()

    def _L0_gnn_setup():
        import jax, jax.numpy as jnp
        import numpy as np
        N_NODES = 3125
        N_EDGES = 100000
        FEAT = 16
        HID = 64
        key = jax.random.key(seed)
        ks = jax.random.split(key, 8)
        x = jax.random.normal(ks[0], (N_NODES, FEAT), dtype=jnp.float32)
        edge_index = jax.random.randint(ks[1], (2, N_EDGES), 0, N_NODES, dtype=jnp.int64)
        W1 = jax.random.normal(ks[2], (FEAT, HID), dtype=jnp.float32) * (1.0 / np.sqrt(FEAT))
        b1 = jax.random.normal(ks[3], (HID,), dtype=jnp.float32) * 0.01
        W2 = jax.random.normal(ks[4], (HID, HID), dtype=jnp.float32) * (1.0 / np.sqrt(HID))
        b2 = jax.random.normal(ks[5], (HID,), dtype=jnp.float32) * 0.01
        W3 = jax.random.normal(ks[6], (HID, FEAT), dtype=jnp.float32) * (1.0 / np.sqrt(HID))
        b3 = jax.random.normal(ks[7], (FEAT,), dtype=jnp.float32) * 0.01
        return {'x': x, 'edge_index': edge_index, 'W1': W1, 'b1': b1, 'W2': W2, 'b2': b2, 'W3': W3, 'b3': b3}
    _L0_gnn_all = _L0_gnn_setup()
    _L0_gnn_in = {k: v for k, v in _L0_gnn_all.items() if k in ('W1', 'b1', 'W2', 'b2', 'W3', 'b3')}
    del _L0_gnn_all

    def _L1_gnn_setup():
        import jax, jax.numpy as jnp
        import numpy as np
        N_NODES = 30000
        N_EDGES = 9375
        IN_FEATS = 16
        OUT_FEATS = 16
        EDGE_DIM = 16
        key = jax.random.key(seed)
        ks = jax.random.split(key, 8)
        feat = jax.random.normal(ks[0], (N_NODES, IN_FEATS), dtype=jnp.float32)
        efeat = jax.random.normal(ks[1], (N_EDGES, EDGE_DIM), dtype=jnp.float32)
        W_msg = jax.random.normal(ks[2], (EDGE_DIM, IN_FEATS * OUT_FEATS), dtype=jnp.float32) * 0.1
        b_msg = jnp.zeros((IN_FEATS * OUT_FEATS,), dtype=jnp.float32)
        W_attn = jax.random.normal(ks[3], (EDGE_DIM, IN_FEATS * OUT_FEATS), dtype=jnp.float32) * 0.1
        b_attn = jnp.zeros((IN_FEATS * OUT_FEATS,), dtype=jnp.float32)
        src = jax.random.randint(ks[4], (N_EDGES,), 0, N_NODES, dtype=jnp.int32)
        dst = jax.random.randint(ks[5], (N_EDGES,), 0, N_NODES, dtype=jnp.int32)
        return {'feat': feat, 'efeat': efeat, 'W_msg': W_msg, 'b_msg': b_msg, 'W_attn': W_attn, 'b_attn': b_attn, 'src': src, 'dst': dst}
    _L1_gnn_all = _L1_gnn_setup()
    _L1_gnn_in = {k: v for k, v in _L1_gnn_all.items() if k in ('W_msg', 'b_msg', 'W_attn', 'b_attn')}
    del _L1_gnn_all
    return {'x': x, 'src': src, 'dst': dst, 'edge_attr_16': edge_attr_16, 'L0_gnn_W1': _L0_gnn_in['W1'], 'L0_gnn_b1': _L0_gnn_in['b1'], 'L0_gnn_W2': _L0_gnn_in['W2'], 'L0_gnn_b2': _L0_gnn_in['b2'], 'L0_gnn_W3': _L0_gnn_in['W3'], 'L0_gnn_b3': _L0_gnn_in['b3'], 'L1_gnn_W_msg': _L1_gnn_in['W_msg'], 'L1_gnn_b_msg': _L1_gnn_in['b_msg'], 'L1_gnn_W_attn': _L1_gnn_in['W_attn'], 'L1_gnn_b_attn': _L1_gnn_in['b_attn']}

def reference(x, src, dst, edge_attr_16, L0_gnn_W1, L0_gnn_b1, L0_gnn_W2, L0_gnn_b2, L0_gnn_W3, L0_gnn_b3, L1_gnn_W_msg, L1_gnn_b_msg, L1_gnn_W_attn, L1_gnn_b_attn):
    import jax
    import jax.numpy as jnp

    def _L0_gnn_ref(x, edge_index, W1, b1, W2, b2, W3, b3):
        import jax, jax.numpy as jnp
        import numpy as np
        N_NODES = 3125
        N_EDGES = 100000
        FEAT = 16
        HID = 64
        N = x.shape[0]
        loops = jnp.arange(N, dtype=edge_index.dtype)
        row = jnp.concatenate([edge_index[0], loops])
        col = jnp.concatenate([edge_index[1], loops])
        deg = jax.ops.segment_sum(jnp.ones_like(col, dtype=x.dtype), col, num_segments=N)
        deg_inv_sqrt = jnp.where(deg > 0, jax.lax.rsqrt(jnp.maximum(deg, 1e-12)), 0.0)
        norm = deg_inv_sqrt[row] * deg_inv_sqrt[col]

        def gcn_layer(h, W, b):
            h = h @ W
            msg = norm[:, None] * h[row]
            agg = jax.ops.segment_sum(msg, col, num_segments=N)
            return agg + b
        h = jax.nn.relu(gcn_layer(x, W1, b1))
        h = jax.nn.relu(gcn_layer(h, W2, b2))
        return gcn_layer(h, W3, b3)

    def _L1_gnn_ref(feat, efeat, W_msg, b_msg, W_attn, b_attn, src, dst):
        import jax, jax.numpy as jnp
        import numpy as np
        N_NODES = 30000
        N_EDGES = 9375
        IN_FEATS = 16
        OUT_FEATS = 16
        EDGE_DIM = 16
        N, in_f = feat.shape
        E = efeat.shape[0]
        w_m = (efeat @ W_msg + b_msg).reshape(E, in_f, -1)
        w_a = (efeat @ W_attn + b_attn).reshape(E, in_f, -1)
        h_src = feat[src][:, :, None]
        e1 = w_m * h_src
        e2 = w_a * h_src
        seg_max = jax.ops.segment_max(e2, dst, num_segments=N)
        ex = jnp.exp(e2 - seg_max[dst])
        denom = jax.ops.segment_sum(ex, dst, num_segments=N)
        attn = ex / denom[dst]
        ft = jax.ops.segment_sum(e1 * attn, dst, num_segments=N)
        return ft.sum(axis=1)
    edge_index = jnp.stack([src, dst])
    x = _layernorm(x + _L0_gnn_ref(x, edge_index, L0_gnn_W1, L0_gnn_b1, L0_gnn_W2, L0_gnn_b2, L0_gnn_W3, L0_gnn_b3), axis=-1)
    x = _layernorm(x + _L1_gnn_ref(x, edge_attr_16, L1_gnn_W_msg, L1_gnn_b_msg, L1_gnn_W_attn, L1_gnn_b_attn, src, dst), axis=-1)
    return x

_drawn_inputs = setup_inputs


def setup_inputs(seed=0):
    import zlib

    import numpy as np

    out = dict(_drawn_inputs(seed))
    spreads = {'L1_gnn_b_msg': (0.0, 0.1), 'L1_gnn_b_attn': (0.0, 0.1)}
    factors = {'L0_gnn_W1': 6.361, 'L0_gnn_b1': 8.0, 'L0_gnn_b2': 8.0, 'L0_gnn_b3': 5.51}
    for name, (base, spread) in spreads.items():
        noise = np.random.default_rng([zlib.crc32(name.encode()), seed]).standard_normal(out[name].shape)
        drawn = base * np.exp(spread * noise) if base else spread * noise
        out[name] = jnp.asarray(drawn.astype(out[name].dtype))
    for name, factor in factors.items():
        out[name] = (out[name] * factor).astype(out[name].dtype)
    return out
```

```python
from contextlib import ExitStack

import concourse.bass as bass
from concourse import mybir

P = 128
F32 = mybir.dt.float32
BF16 = mybir.dt.bfloat16
I32 = mybir.dt.int32
ALU = mybir.AluOpType
ACT = mybir.ActivationFunctionType
AX_X = mybir.AxisListType.X
RMAX = bass.bass_isa.ReduceOp.max

N = 3125
E = 103125
FEAT = 16
HID = 64
CH = FEAT * FEAT
NT = -(-(N + 1) // P)
NT += NT % 2
NP = NT * P
NPAIR = NT // 2
PAD = NP
NB = -(-E // P)
SLOT = 8
EP = E + SLOT
FAR = 4096
CAP = 4000
TERMS = 6
KROWS = TERMS * FEAT + 4
MASKED = -1e30
EPS = 1e-5


def gnn_kernel(nc, x, src, dst, edge_attr, W1, b1, W2, b2, W3, b3, W_msg, b_msg, W_attn, b_attn, out):
    rec = nc.dram_tensor("node_records", [NP, 4], I32, kind="Internal").ap()
    key_row = nc.dram_tensor("key_row", [NP], F32, kind="Internal").ap()
    table = [nc.dram_tensor(f"table{i}", [PAD + 1, f], F32, kind="Internal").ap()
             for i, f in enumerate((FEAT, HID, HID, FEAT))]
    out_pad = nc.dram_tensor("out_pad", [NP, FEAT], F32, kind="Internal").ap()

    with ExitStack() as ctx:
        def sb(name, shape, dt=F32):
            return ctx.enter_context(nc.sbuf_tensor(name, shape, dt))

        def sem(name):
            return ctx.enter_context(nc.semaphore(name))

        ident = sb("ident", [P, P])
        identb = sb("identb", [P, P], BF16)
        ones_row = sb("ones_row", [1, P])
        slot_no = sb("slot_no", [P, 2, SLOT])
        node_i = sb("node_i", [P, NT + 1], I32)
        node_f = sb("node_f", [P, NT + 1])
        firsts_i = sb("firsts_i", [1, NB], I32)
        firsts_r = sb("firsts_r", [1, NB])
        firsts = sb("firsts", [P, NB])
        junk = sb("junk", [P, NP])
        key_all = sb("key_all", [P, NP])
        blk_f = sb("blk_f", [P, NT + 1])
        blk_i = sb("blk_i", [P, NT + 1], I32)
        dst_blk = sb("dst_blk", [P, NT + 1, P], I32)
        below = sb("below", [P, NT + 1])
        rowptr = sb("rowptr", [P, NT + 1])
        deg_n = sb("deg_n", [P, NT])
        key = sb("key", [P, NT])
        rank_f = sb("rank_f", [P, NT])
        rank_i = sb("rank_i", [P, NT], I32)
        rec_n = sb("rec_n", [P, NT, 4], I32)
        rec_p = sb("rec_p", [P, NT, 4], I32)
        ids = sb("ids", [P, NT], I32)
        start_p = sb("start_p", [P, NT], I32)
        deg_p = sb("deg_p", [P, NT])
        has_edge = sb("has_edge", [P, NT])
        dinv = sb("dinv", [P, NT])
        deg_max = sb("deg_max", [P, NT])
        lev_f = sb("lev_f", [1, NPAIR])
        lev_i = sb("lev_i", [1, NPAIR], I32)
        levels = sb("levels", [1, NPAIR + 1], I32)
        lev_sum = sb("lev_sum", [1, 1])
        one_col = sb("one_col", [P, 1])
        eps_col = sb("eps_col", [P, 1])
        xp = sb("xp", [P, NT, FEAT])
        gfeat = sb("gfeat", [P, NT, HID])
        agg = sb("agg", [P, NT, HID])
        part = [sb(f"part{h}", [P, HID]) for h in range(2)]
        z = sb("z", [P, 2, HID])
        zT = sb("zT", [HID + 1, 2 * P])
        wb = [sb("w1b", [FEAT + 1, HID]), sb("w2b", [HID + 1, HID]), sb("w3b", [HID + 1, FEAT])]
        x1 = sb("x1", [P, NT, FEAT])
        cen = sb("cen", [P, NT, FEAT])
        sq = sb("sq", [P, NT, FEAT])
        stat = sb("stat", [P, NT])
        pad_row = sb("pad_row", [1, 2 * HID])
        cursor = sb("cursor", [P, 2], I32)
        remain = sb("remain", [P, 2])
        src_run = [sb(f"src_run{h}", [P, SLOT], I32) for h in range(2)]
        src_rel = sb("src_rel", [P, 2, SLOT])
        used_slot = sb("used_slot", [P, 2, SLOT])
        slot_idx = sb("slot_idx", [P, 2 * SLOT], I32)
        nbr = [sb(f"nbr{h}", [P, SLOT * HID]) for h in range(2)]
        attr = [sb(f"attr{h}", [P, SLOT * FEAT]) for h in range(2)]
        hole = [sb(f"hole{h}", [P, SLOT]) for h in range(2)]
        wf = sb("wf", [P, 2 * CH])
        wres = sb("wres", [P, 2 * CH])
        wsplit = sb("wsplit", [FEAT, 3, 2 * CH], BF16)
        bsplit = sb("bsplit", [1, 3, 2 * CH], BF16)
        bf = sb("bf", [1, 2 * CH])
        bres = sb("bres", [1, 2 * CH])
        mask_w = sb("mask_w", [1, 2 * CH], BF16)
        wk = sb("wk", [KROWS, 2 * CH], BF16)
        terms = [sb(f"terms{h}", [P, SLOT, KROWS], BF16) for h in range(2)]
        res1 = sb("res1", [P, SLOT, FEAT])
        termsT = [sb(f"termsT{h}", [KROWS, SLOT * P], BF16) for h in range(2)]
        e2 = [sb(f"e2{h}", [P, SLOT, CH]) for h in range(2)]
        exm = [sb(f"exm{h}", [P, SLOT, 2 * CH]) for h in range(2)]
        e1 = sb("e1", [P, SLOT, CH])
        cmax = sb("cmax", [P, CH])
        peak = [sb(f"peak{h}", [P, CH]) for h in range(2)]
        mdiff = sb("mdiff", [P, CH])
        fade = [sb(f"fade{h}", [P, CH]) for h in range(2)]
        acc = [sb(f"acc{h}", [P, 2, CH]) for h in range(2)]
        rden = sb("rden", [P, CH])
        ratio = sb("ratio", [P, CH])
        ft = sb("ft", [P, FEAT])
        x2 = sb("x2", [P, NT, FEAT])

        bank = [ctx.enter_context(nc.psum_tensor(f"bank{i}", [P, 512], F32)) for i in range(2)]
        pw = ctx.enter_context(nc.psum_tensor("pw", [P, 4, 512], F32))
        pt = ctx.enter_context(nc.psum_tensor("pt", [P, SLOT * P], BF16))
        psum_acc = ctx.enter_context(nc.psum_tensor("psum_acc", [P, 2 * CH], F32))

        s_in = sem("s_in")
        s_wk = sem("s_wk")
        s_const = sem("s_const")
        s_frow = sem("s_frow")
        s_fbc = sem("s_fbc")
        s_blk = sem("s_blk")
        s_dblk = sem("s_dblk")
        s_key = sem("s_key")
        s_keyd = sem("s_keyd")
        s_keyb = sem("s_keyb")
        s_rank = sem("s_rank")
        s_recd = sem("s_recd")
        s_recp = sem("s_recp")
        s_place = sem("s_place")
        s_dmax = sem("s_dmax")
        s_lev = sem("s_lev")
        s_sqrt_in = sem("s_sqrt_in")
        s_sqrt = sem("s_sqrt")
        s_xp = sem("s_xp")
        s_wsp = sem("s_wsp")
        s_pads = sem("s_pads")
        s_padz = sem("s_padz")
        s_g = sem("s_g")
        s_tab = sem("s_tab")
        s_z = sem("s_z")
        s_zt = sem("s_zt")
        s_ztc = sem("s_ztc")
        s_mm = sem("s_mm")
        s_h = sem("s_h")
        s_pool = sem("s_pool")
        s_srun = sem("s_srun")
        s_settled = sem("s_settled")
        s_settled_pe = sem("s_settled_pe")
        c_srun = sem("c_srun")
        c_nbr = [sem(f"c_nbr{h}") for h in range(2)]
        c_nbr_free = [sem(f"c_nbr_free{h}") for h in range(2)]
        s_nbr = [sem(f"s_nbr{h}") for h in range(2)]
        s_nbr_free = [sem(f"s_nbr_free{h}") for h in range(2)]
        s_attr = [sem(f"s_attr{h}") for h in range(2)]
        s_attr_free = [sem(f"s_attr_free{h}") for h in range(2)]
        s_hole = sem("s_hole")
        s_hi = sem("s_hi")
        s_mid = sem("s_mid")
        s_r1 = sem("s_r1")
        s_lo = sem("s_lo")
        s_tT = sem("s_tT")
        s_tTc = sem("s_tTc")
        s_w = sem("s_w")
        s_wfree = sem("s_wfree")
        s_d = sem("s_d")
        s_ex = sem("s_ex")
        s_md = sem("s_md")
        s_fade = sem("s_fade")
        s_p = sem("s_p")
        s_sum = sem("s_sum")
        s_accd = sem("s_accd")
        s_var = sem("s_var")
        s_std = sem("s_std")
        s_x2 = sem("s_x2")
        s_out = sem("s_out")
        s_final = sem("s_final")

        GCN_TABLES = (0, 1, 2)
        FIN = (FEAT, HID, HID)
        FOUT = (HID, HID, FEAT)

        src_rows = src.rearrange("(e a) -> e a", a=1)
        dst_blocks = dst.rearrange("(b p) -> b p", p=P)

        block = ctx.enter_context(nc.Block())

        @block.sync
        def _(sp):
            sp.dma_start(firsts_i[:], dst_blocks[:, 0:1].rearrange("b a -> a b"), allow_slow_non_contiguous=True).then_inc(s_in, 16)
            sp.dma_start(wb[0][0:FEAT, :], W1).then_inc(s_in, 16)
            sp.dma_start(wb[0][FEAT:FEAT + 1, :], b1.rearrange("(a n) -> a n", a=1)).then_inc(s_in, 16)
            sp.dma_start(wb[1][0:HID, :], W2).then_inc(s_in, 16)
            sp.dma_start(wb[1][HID:HID + 1, :], b2.rearrange("(a n) -> a n", a=1)).then_inc(s_in, 16)
            sp.dma_start(wb[2][0:HID, :], W3).then_inc(s_in, 16)
            sp.dma_start(wb[2][HID:HID + 1, :], b3.rearrange("(a n) -> a n", a=1)).then_inc(s_in, 16)
            sp.dma_start(wf[0:FEAT, 0:CH], W_attn).then_inc(s_in, 16)
            sp.dma_start(wf[0:FEAT, CH:2 * CH], W_msg).then_inc(s_in, 16)
            sp.dma_start(bf[:, 0:CH], b_attn.rearrange("(a n) -> a n", a=1)).then_inc(s_in, 16)
            sp.dma_start(bf[:, CH:2 * CH], b_msg.rearrange("(a n) -> a n", a=1)).then_inc(s_in, 16)
            sp.wait_ge(s_padz, 1)
            for i in range(3):
                f = table[i].shape[1]
                sp.dma_start(table[i][PAD:PAD + 1, :], pad_row[:, 0:f]).then_inc(s_pads, 16)
            sp.dma_start(table[3][PAD:PAD + 1, :], pad_row[:, HID:HID + FEAT]).then_inc(s_pads, 16)
            sp.wait_ge(s_wsp, 1)
            for t, k in enumerate((0, 1, 2, 0, 1, 0)):
                sp.dma_start(wk[t * FEAT:(t + 1) * FEAT, :], wsplit[:, k, :]).then_inc(s_wk, 16)
            for k in range(3):
                sp.dma_start(wk[TERMS * FEAT + k:TERMS * FEAT + k + 1, :], bsplit[:, k, :]).then_inc(s_wk, 16)
            sp.dma_start(wk[KROWS - 1:KROWS, :], mask_w[:]).then_inc(s_wk, 16)
            sp.wait_ge(s_key, 1)
            sp.dma_start(key_row.rearrange("(p t) -> p t", p=P), key[:]).then_inc(s_keyd, 16)
            sp.wait_ge(s_keyd, 16)
            sp.dma_start(key_all[:], key_row.rearrange("(a n) -> a n", a=1).broadcast_to([P, NP])).then_inc(s_keyb, 16)
            sp.wait_ge(s_recd, 16 * NT)
            sp.dma_start(rec_p[:], rec.rearrange("(t p) c -> p t c", p=P)).then_inc(s_recp, 16)
            sp.wait_ge(s_x2, 1)
            sp.wait_ge(s_out, 16 * NT)
            sp.dma_start(out, out_pad[0:N, :]).then_inc(s_final, 16)
            sp.wait_ge(s_final, 16)
            sp.wait_ge(s_pads, 64)

        @block.gpsimd
        def _(pool):
            pool.memset(ident[:], 0.0)
            pool.memset(identb[:], 0.0)
            pool.memset(ones_row[:], 1.0)
            pool.iota(node_i[:], pattern=[[1, NT + 1]], base=0, channel_multiplier=NT)
            pool.iota(slot_no[:], pattern=[[0, 2], [1, SLOT]], base=0, channel_multiplier=0,
                      allow_small_or_imprecise_dtypes=True)
            pool.drain()
            for m in (ident, identb):
                pool.affine_select(out=m[:], in_=m[:], compare_op=ALU.not_equal, fill=1.0, base=0,
                                   pattern=[[-1, P]], channel_multiplier=1)
            pool.drain().then_inc(s_const, 1)
            pool.wait_ge(s_blk, 1)
            for t in range(NT + 1):
                pool.indirect_dma_start(dst_blk[:, t, :], None, dst_blocks,
                                        bass.IndirectOffsetOnAxis(ap=blk_i[:, t:t + 1], axis=0)).then_inc(s_dblk, 16)
            pool.wait_ge(s_rank, 1)
            for t in range(NT):
                pool.indirect_dma_start(rec, bass.IndirectOffsetOnAxis(ap=rank_i[:, t:t + 1], axis=0),
                                        rec_n[:, t, :], None).then_inc(s_recd, 16)
            pool.wait_ge(s_place, 1)
            pool.partition_all_reduce(deg_max[:], deg_p[:], P, RMAX).then_inc(s_dmax, 1)
            for t in range(NT):
                pool.indirect_dma_start(xp[:, t, :], None, x,
                                        bass.IndirectOffsetOnAxis(ap=ids[:, t:t + 1], axis=0)).then_inc(s_xp, 16)

            def write_table(k, rows, f):
                pool.wait_ge(s_g, k + 1)
                for t in range(NT):
                    pool.indirect_dma_start(table[k], bass.IndirectOffsetOnAxis(ap=ids[:, t:t + 1], axis=0),
                                            rows[:, t, 0:f], None).then_inc(s_tab, 16)
                pool.wait_ge(s_tab, 16 * NT * (k + 1))

            step = pool.alloc_register("pool_step")

            def wait(s, value):
                pool.wait_ge(s, value)
                pool.sem_inc(s_settled, 1)

            def run_gather(dst_tile, table_ap, h, signal):
                pool.indirect_dma_start(dst_tile[:], None, table_ap,
                                        bass.IndirectOffsetOnAxis(ap=cursor[:, h:h + 1], axis=0)).then_inc(signal, 16)

            def start_pair(q):
                pool.tensor_copy(cursor[:], start_p[:, bass.ds(q * 2, 2)])
                pool.tensor_copy(remain[:], deg_p[:, bass.ds(q * 2, 2)])
                pool.drain()

            def slot_indices(srun_signal, srun_value):
                pool.tensor_tensor(used_slot[:], remain[:].unsqueeze(2).broadcast_to([P, 2, SLOT]), slot_no[:],
                                   ALU.subtract)
                pool.drain()
                pool.tensor_scalar(used_slot[:], used_slot[:], 0.0, 1.0, ALU.max, ALU.min)
                wait(srun_signal, srun_value)
                for h in range(2):
                    pool.tensor_scalar(src_rel[:, h, :], src_run[h][:], float(PAD), None, ALU.subtract)
                pool.drain()
                pool.tensor_tensor(src_rel[:], src_rel[:], used_slot[:], ALU.mult)
                pool.drain()
                pool.tensor_scalar(slot_idx[:], src_rel[:].rearrange("p h s -> p (h s)"), float(PAD), None, ALU.add)
                pool.tensor_scalar(cursor[:], cursor[:], float(SLOT), float(E), ALU.add, ALU.min)
                pool.tensor_scalar(remain[:], remain[:], float(SLOT), None, ALU.subtract)

            def row_gathers(k, f, h, signal):
                for j in range(SLOT):
                    c = h * SLOT + j
                    pool.indirect_dma_start(nbr[h][:, j * f:(j + 1) * f], None, table[k],
                                            bass.IndirectOffsetOnAxis(ap=slot_idx[:, c:c + 1], axis=0)
                                            ).then_inc(signal, 16)

            pool.reg_mov(step, 0)
            pool.wait_ge(s_lev, 1)
            pool.wait_ge(s_pads, 64)
            for k in range(3):
                write_table(k, gfeat, FIN[k])
                with pool.Fori(0, NPAIR) as q:
                    n = pool.value_load(levels[0:1, bass.ds(q, 1)], min_val=1, max_val=E)
                    start_pair(q)
                    with pool.Fori(0, n) as _level:
                        g = pool.snap(step, min_val=0, max_val=1 << 16)
                        for h in range(2):
                            run_gather(src_run[h], src_rows, h, c_srun)
                        slot_indices(c_srun, g * 32 + 32)
                        pool.drain()
                        for h in range(2):
                            wait(c_nbr_free[h], g + 1)
                            row_gathers(k, FIN[k], h, c_nbr[h])
                        pool.reg_add(step, step, 1)

            write_table(3, x1, FEAT)
            pool.reg_mov(step, 0)
            with pool.Fori(0, NPAIR) as q:
                n = pool.value_load(levels[0:1, bass.ds(q, 1)], min_val=1, max_val=E)
                start_pair(q)
                with pool.Fori(0, n) as _level:
                    g = pool.snap(step, min_val=0, max_val=1 << 16)
                    for h in range(2):
                        run_gather(src_run[h], src_rows, h, s_srun)
                    for h in range(2):
                        wait(s_attr_free[h], g + 1)
                        run_gather(attr[h], edge_attr, h, s_attr[h])
                    slot_indices(s_srun, g * 32 + 32)
                    for h in range(2):
                        pool.tensor_scalar(hole[h][:], used_slot[:, h, :], -1.0, 1.0, ALU.mult, ALU.add)
                    pool.drain().then_inc(s_hole, 1)
                    for h in range(2):
                        wait(s_nbr_free[h], g + 1)
                        row_gathers(3, FEAT, h, s_nbr[h])
                    pool.reg_add(step, step, 1)
            g = pool.snap(step, min_val=0, max_val=1 << 16)
            wait(s_attr_free[0], g + 1)
            run_gather(attr[0], edge_attr, 0, s_attr[0])
            pool.nop().then_inc(s_hole, 1)
            pool.wait_ge(s_x2, 1)
            for t in range(NT):
                pool.indirect_dma_start(out_pad, bass.IndirectOffsetOnAxis(ap=ids[:, t:t + 1], axis=0),
                                        x2[:, t, :], None).then_inc(s_out, 16)
            pool.wait_ge(s_out, 16 * NT)

        @block.tensor
        def _(pe):
            pe.wait_ge(s_const, 1)
            pe.wait_ge(s_frow, 1)
            half = NB // 2
            for i in range(2):
                mm = pe.matmul(bank[i][:, 0:half], ones_row[:], firsts_r[:, i * half:(i + 1) * half],
                               start=True, stop=True)
            mm.then_inc(s_fbc, 1)

            step = pe.alloc_register("pe_step")
            pe.reg_mov(step, 0)
            pe.wait_ge(s_in, 16 * 11)
            for k in range(3):
                with pe.Fori(0, NPAIR) as _q:
                    g = pe.snap(step, min_val=0, max_val=1 << 12)
                    pe.wait_ge(s_z, g + 1)
                    pe.sem_inc(s_settled_pe, 1)
                    for h in range(2):
                        mm = pe.transpose(bank[0][0:FIN[k], h * P:(h + 1) * P], z[:, h, 0:FIN[k]], ident[:])
                    mm.then_inc(s_zt, 1)
                    pe.wait_ge(s_ztc, g + 1)
                    pe.wait_ge(s_h, g + 1)
                    for h in range(2):
                        mm = pe.matmul(bank[1][:, h * HID:h * HID + FOUT[k]], zT[0:FIN[k] + 1, h * P:(h + 1) * P],
                                       wb[k][:], start=True, stop=True)
                    mm.then_inc(s_mm, 1)
                    pe.reg_add(step, step, 1)

            def turn(h, v):
                pe.wait_ge(s_lo, v)
                pe.wait_ge(s_tTc, v)
                for j in range(SLOT):
                    mm = pe.transpose(pt[0:KROWS, j * P:(j + 1) * P], terms[h][:, j, :], identb[:])
                mm.then_inc(s_tT, 1)

            def product(h, m, value):
                for i in range(2):
                    pe.wait_ge(s_wfree, value + i)
                    for j in range(4 * i, 4 * i + 4):
                        mm = pe.matmul(pw[:, 2 * i + j % 4 // 2, (j % 2) * CH:(j % 2 + 1) * CH],
                                       termsT[h][:, j * P:(j + 1) * P], wk[:, m * CH:(m + 1) * CH],
                                       start=True, stop=True)
                    mm.then_inc(s_w, 1)

            def sums(h, v):
                pe.wait_ge(s_p, v)
                pe.wait_ge(s_accd, v)
                for j in range(SLOT):
                    mm = pe.matmul(psum_acc[:], ident[:], exm[h][:, j, :], start=(j == 0), stop=(j == SLOT - 1))
                mm.then_inc(s_sum, 1)

            pe.wait_ge(s_wk, 16 * (TERMS + 4))
            pe.reg_mov(step, 0)
            turn(0, 1)
            pe.wait_ge(s_tTc, 2)
            product(0, 0, 1)
            total = pe.value_load(levels[0:1, NPAIR:NPAIR + 1], min_val=1, max_val=1 << 16)
            with pe.Fori(0, total) as _s:
                g = pe.snap(step, min_val=0, max_val=1 << 16)
                for h in range(2):
                    product(h, 1, g * 8 + 4 * h + 3)
                    turn(1 - h, g * 2 + h + 2)
                    pe.wait_ge(s_tTc, g * 2 + h + 3)
                    product(1 - h, 0, g * 8 + 4 * h + 5)
                    sums(h, g * 2 + h + 1)
                pe.reg_add(step, step, 1)

        @block.scalar
        def _(act):
            act.wait_ge(s_sqrt_in, 1)
            act.activation(dinv[:], deg_p[:], ACT.Sqrt, bias=one_col[:]).then_inc(s_sqrt, 1)
            step = act.alloc_register("act_step")
            act.reg_mov(step, 0)
            for k in range(3):
                with act.Fori(0, NPAIR) as _q:
                    g = act.snap(step, min_val=0, max_val=1 << 12)
                    act.wait_ge(s_zt, g + 1)
                    act.copy(zT[0:FIN[k], :], bank[0][0:FIN[k], 0:2 * P]).then_inc(s_ztc, 1)
                    act.reg_add(step, step, 1)
            act.wait_ge(s_var, 1)
            act.activation(stat[:], stat[:], ACT.Sqrt, bias=eps_col[:]).then_inc(s_std, 1)

            def high(h, value):
                act.wait_ge(s_attr[h], value)
                act.copy(terms[h][:, :, 0:3 * FEAT].rearrange("p s (t f) -> p s t f", t=3),
                         attr[h][:].rearrange("p (s f) -> p s f", s=SLOT).unsqueeze(2)
                         .broadcast_to([P, SLOT, 3, FEAT])).then_inc(s_hi, 1)

            def middle(h, v):
                act.wait_ge(s_r1, v)
                act.copy(terms[h][:, :, 3 * FEAT:5 * FEAT].rearrange("p s (t f) -> p s t f", t=2),
                         res1[:].unsqueeze(2).broadcast_to([P, SLOT, 2, FEAT])).then_inc(s_mid, 1)

            def turned(h, v):
                act.wait_ge(s_tT, v)
                act.copy(termsT[h][:], pt[0:KROWS, :]).then_inc(s_tTc, 1)

            act.sem_inc(s_tTc, 1)
            act.reg_mov(step, 0)
            high(0, 16)
            middle(0, 1)
            turned(0, 1)
            total = act.value_load(levels[0:1, NPAIR:NPAIR + 1], min_val=1, max_val=1 << 16)
            with act.Fori(0, total) as _s:
                g = act.snap(step, min_val=0, max_val=1 << 16)
                for h in range(2):
                    high(1 - h, g * 16 + 16 + 16 * h)
                    act.wait_ge(s_md, g * 2 + h + 1)
                    act.activation(fade[h][:], mdiff[:], ACT.Exp).then_inc(s_fade, 1)
                    act.wait_ge(s_d, g * 2 + h + 1)
                    act.wait_ge(s_sum, g * 2 + h + 1)
                    act.activation(exm[h][:, :, 0:CH], e2[h][:], ACT.Exp).then_inc(s_ex, 1)
                    middle(1 - h, g * 2 + h + 2)
                    turned(1 - h, g * 2 + h + 2)
                act.reg_add(step, step, 1)
            act.wait_ge(s_var, 2)
            act.activation(stat[:], stat[:], ACT.Sqrt, bias=eps_col[:]).then_inc(s_std, 1)

        @block.vector
        def _(dve):
            dve.memset(pad_row[:, 0:HID], 0.0)
            dve.memset(pad_row[:, HID:2 * HID], 1.0).then_inc(s_padz, 1)
            dve.memset(one_col[:], 1.0)
            dve.memset(eps_col[:], EPS)
            dve.memset(zT[:], 1.0)
            dve.memset(mask_w[:, 0:CH], MASKED)
            dve.memset(mask_w[:, CH:2 * CH], 0.0)
            for h in range(2):
                dve.memset(terms[h][:, :, TERMS * FEAT:KROWS], 1.0)
            for s in (*c_nbr_free, *s_attr_free, *s_nbr_free, s_h, s_accd):
                dve.sem_inc(s, 1)
            for s in (s_wfree, s_sum):
                dve.sem_inc(s, 2)

            dve.wait_ge(s_in, 16 * 11)
            dve.tensor_copy(firsts_r[:], firsts_i[:]).then_inc(s_frow, 1)
            for full, rest, part3 in ((wf[0:FEAT, :], wres[0:FEAT, :], wsplit), (bf[:], bres[:], bsplit)):
                dve.tensor_copy(part3[:, 0, :], full)
                dve.drain()
                dve.tensor_tensor(rest, full, part3[:, 0, :], ALU.subtract)
                dve.drain()
                dve.tensor_copy(part3[:, 1, :], rest)
                dve.drain()
                dve.tensor_tensor(part3[:, 2, :], rest, part3[:, 1, :], ALU.subtract)
            dve.drain().then_inc(s_wsp, 1)

            dve.wait_ge(s_const, 1)
            dve.tensor_copy(node_f[:], node_i[:])
            dve.wait_ge(s_fbc, 1)
            half = NB // 2
            for i in range(2):
                dve.tensor_copy(firsts[:, i * half:(i + 1) * half], bank[i][:, 0:half])
            dve.drain()
            for t in range(NT + 1):
                dve.tensor_scalar(junk[:, 0:NB], firsts[:], node_f[:, t:t + 1], 0.0, ALU.is_lt, ALU.add,
                                  accum_out=blk_f[:, t:t + 1])
                dve.drain()
            dve.drain()
            dve.tensor_scalar(blk_f[:], blk_f[:], -1.0, 0.0, ALU.add, ALU.max)
            dve.drain()
            dve.tensor_copy(blk_i[:], blk_f[:]).then_inc(s_blk, 1)
            dve.wait_ge(s_dblk, 16 * (NT + 1))
            for t in range(NT + 1):
                dve.tensor_scalar(junk[:, 0:P], dst_blk[:, t, :], node_f[:, t:t + 1], 0.0, ALU.is_lt, ALU.add,
                                  accum_out=below[:, t:t + 1])
                dve.drain()
            dve.drain()
            dve.scalar_tensor_tensor(out=rowptr[:], in0=blk_f[:], scalar=float(P), in1=below[:],
                                     op0=ALU.mult, op1=ALU.add)
            dve.drain()
            dve.tensor_tensor(deg_n[:], rowptr[:, 1:NT + 1], rowptr[:, 0:NT], ALU.subtract)
            dve.drain()
            dve.tensor_scalar(key[:], deg_n[:], float(CAP), 4096.0, ALU.min, ALU.mult)
            dve.drain()
            dve.tensor_tensor(key[:], key[:], node_f[:, 0:NT], ALU.subtract)
            dve.drain()
            dve.tensor_scalar(key[:], key[:], float(NP - 1), None, ALU.add)
            dve.drain().then_inc(s_key, 1)
            dve.tensor_copy(rec_n[:, :, 0], node_i[:, 0:NT])
            dve.tensor_copy(rec_n[:, :, 1], rowptr[:, 0:NT])
            dve.tensor_copy(rec_n[:, :, 2], deg_n[:])
            dve.tensor_copy(rec_n[:, :, 3], deg_n[:])
            dve.wait_ge(s_keyb, 16)
            for t in range(NT):
                dve.tensor_scalar(junk[:], key_all[:], key[:, t:t + 1], 0.0, ALU.is_gt, ALU.add,
                                  accum_out=rank_f[:, t:t + 1])
                dve.drain()
            dve.drain()
            dve.tensor_copy(rank_i[:], rank_f[:])
            dve.drain().then_inc(s_rank, 1)

            dve.wait_ge(s_recp, 16)
            dve.tensor_copy(ids[:], rec_p[:, :, 0])
            dve.tensor_copy(start_p[:], rec_p[:, :, 1])
            dve.tensor_copy(deg_p[:], rec_p[:, :, 2])
            dve.drain().then_inc(s_sqrt_in, 1)
            dve.drain().then_inc(s_place, 1)
            dve.tensor_scalar(has_edge[:], deg_p[:], 1.0, None, ALU.min)
            dve.wait_ge(s_dmax, 1)
            dm = deg_max[0:1, :].rearrange("a (q h) -> a q h", h=2)
            dve.tensor_tensor(lev_f[:, 0:NPAIR], dm[:, :, 0], dm[:, :, 1], ALU.max)
            dve.drain()
            dve.tensor_scalar(lev_f[:, 0:NPAIR], lev_f[:, 0:NPAIR], float(SLOT - 1), float(SLOT), ALU.add, ALU.max)
            dve.drain()
            dve.tensor_copy(lev_i[:], lev_f[:])
            dve.drain()
            dve.tensor_scalar(levels[:, 0:NPAIR], lev_i[:], SLOT.bit_length() - 1, None, ALU.logical_shift_right)
            dve.drain()
            dve.tensor_copy(lev_f[:], levels[:, 0:NPAIR])
            dve.drain()
            dve.tensor_reduce(lev_sum[:], lev_f[:], AX_X, ALU.add)
            dve.drain()
            dve.tensor_copy(levels[:, NPAIR:NPAIR + 1], lev_sum[:])
            dve.drain().then_inc(s_lev, 1)

            dve.wait_ge(s_sqrt, 1)
            dve.reciprocal(dinv[:], dinv[:])
            dve.wait_ge(s_xp, 16 * NT)
            dve.drain()
            dve.tensor_tensor(gfeat[:, :, 0:FEAT], xp[:], dinv[:].unsqueeze(2).broadcast_to([P, NT, FEAT]), ALU.mult)
            dve.drain().then_inc(s_g, 1)

            step = dve.alloc_register("dve_step")
            pair = dve.alloc_register("dve_pair")
            dve.reg_mov(step, 0)
            dve.reg_mov(pair, 0)
            for k in range(3):
                f, fo = FIN[k], FOUT[k]
                dve.memset(agg[:], 0.0)
                dve.drain()
                with dve.Fori(0, NPAIR) as q:
                    n = dve.value_load(levels[0:1, bass.ds(q, 1)], min_val=1, max_val=E)
                    with dve.Fori(0, n) as _level:
                        g = dve.snap(step, min_val=0, max_val=1 << 16)
                        for h in range(2):
                            dve.wait_ge(c_nbr[h], g * 16 * SLOT + 16 * SLOT)
                            dve.tensor_reduce(part[h][:, 0:f], nbr[h][:, 0:SLOT * f]
                                              .rearrange("p (s f) -> p f s", s=SLOT), AX_X, ALU.add
                                              ).then_inc(c_nbr_free[h], 1)
                        dve.drain()
                        for h in range(2):
                            at = agg[:, bass.ds(q * 2 + h, 1), 0:f]
                            dve.tensor_tensor(at, at, part[h][:, 0:f].unsqueeze(1), ALU.add)
                        dve.drain()
                        dve.reg_add(step, step, 1)
                with dve.Fori(0, NPAIR) as q:
                    g = dve.snap(pair, min_val=0, max_val=1 << 12)
                    tiles = bass.ds(q * 2, 2)
                    dve.tensor_tensor(z[:, :, 0:f], agg[:, tiles, 0:f], gfeat[:, tiles, 0:f], ALU.add)
                    dve.drain()
                    dve.tensor_tensor(z[:, :, 0:f], z[:, :, 0:f],
                                      dinv[:, tiles].unsqueeze(2).broadcast_to([P, 2, f]), ALU.mult
                                      ).then_inc(s_z, 1)
                    dve.wait_ge(s_mm, g + 1)
                    for h in range(2):
                        res = bank[1][:, h * HID:h * HID + fo]
                        if k < 2:
                            op = dve.tensor_scalar(gfeat[:, bass.ds(q * 2 + h, 1), :].rearrange("p a f -> p (a f)"), res, 0.0,
                                                   dinv[:, bass.ds(q * 2 + h, 1)], ALU.max, ALU.mult)
                        else:
                            op = dve.tensor_tensor(x1[:, bass.ds(q * 2 + h, 1), :].rearrange("p a f -> p (a f)"), res,
                                                   xp[:, bass.ds(q * 2 + h, 1), :].rearrange("p a f -> p (a f)"), ALU.add)
                    op.then_inc(s_h, 1)
                    dve.reg_add(pair, pair, 1)
                if k < 2:
                    dve.drain().then_inc(s_g, 1)

            def layernorm(v, count):
                wide = [P, NT, FEAT]
                dve.drain()
                dve.tensor_reduce(stat[:], v[:], AX_X, ALU.add)
                dve.drain()
                dve.tensor_scalar(stat[:], stat[:], 1.0 / FEAT, None, ALU.mult)
                dve.drain()
                dve.tensor_tensor(v[:], v[:], stat[:].unsqueeze(2).broadcast_to(wide), ALU.subtract)
                dve.drain()
                dve.tensor_tensor(sq[:], v[:], v[:], ALU.mult)
                dve.drain()
                dve.tensor_reduce(stat[:], sq[:], AX_X, ALU.add)
                dve.drain()
                dve.tensor_scalar(stat[:], stat[:], 1.0 / FEAT, None, ALU.mult).then_inc(s_var, 1)
                dve.wait_ge(s_std, count)
                dve.reciprocal(stat[:], stat[:])
                dve.drain()
                dve.tensor_tensor(v[:], v[:], stat[:].unsqueeze(2).broadcast_to(wide), ALU.mult)

            layernorm(x1, 1)
            dve.drain().then_inc(s_g, 1)

            def rest_one(h, hole_value, v):
                dve.wait_ge(s_hole, hole_value)
                dve.wait_ge(s_hi, v)
                dve.tensor_copy(terms[h][:, :, KROWS - 1:KROWS].rearrange("p s a -> p (s a)"), hole[h][:])
                dve.tensor_tensor(res1[:], attr[h][:].rearrange("p (s f) -> p s f", s=SLOT),
                                  terms[h][:, :, 0:FEAT], ALU.subtract).then_inc(s_r1, 1)
                dve.drain().then_inc(s_attr_free[h], 1)

            def rest_two(h, v):
                dve.wait_ge(s_mid, v)
                dve.tensor_tensor(terms[h][:, :, 5 * FEAT:6 * FEAT], res1[:], terms[h][:, :, 3 * FEAT:4 * FEAT],
                                  ALU.subtract)
                dve.drain().then_inc(s_lo, 1)

            def scaled(to, h, value):
                for i in range(2):
                    dve.wait_ge(s_w, value + i)
                    h_src = nbr[h][:, 4 * i * FEAT:(4 * i + 4) * FEAT].unsqueeze(2)
                    dve.tensor_tensor(to[:, 4 * i:4 * i + 4, :].rearrange("p s (i o) -> p (s i) o", o=FEAT),
                                      pw[:, 2 * i:2 * i + 2, :].rearrange("p b (s i o) -> p (b s i) o", s=2, o=FEAT),
                                      h_src.broadcast_to([P, 4 * FEAT, FEAT]), ALU.mult).then_inc(s_wfree, 1)

            def accumulate(h, v):
                dve.wait_ge(s_sum, v)
                dve.tensor_tensor(acc[h][:], acc[h][:], fade[h][:].unsqueeze(1).broadcast_to([P, 2, CH]), ALU.mult)
                dve.drain()
                dve.tensor_tensor(acc[h][:].rearrange("p a c -> p (a c)"), acc[h][:].rearrange("p a c -> p (a c)"),
                                  psum_acc[:], ALU.add)
                dve.drain().then_inc(s_accd, 1)

            dve.reg_mov(step, 0)
            rest_one(0, 1, 1)
            rest_two(0, 1)
            with dve.Fori(0, NPAIR) as q:
                n = dve.value_load(levels[0:1, bass.ds(q, 1)], min_val=1, max_val=E)
                for h in range(2):
                    dve.memset(peak[h][:], -3e38)
                    dve.memset(acc[h][:], 0.0)
                dve.drain()
                with dve.Fori(0, n) as level:
                    g = dve.snap(step, min_val=0, max_val=1 << 16)
                    for h in range(2):
                        dve.wait_ge(s_nbr[h], g * 16 * SLOT + 16 * SLOT)
                        scaled(e2[h], h, g * 8 + 4 * h + 1)
                        dve.drain()
                        dve.tensor_reduce(cmax[:], e2[h][:].rearrange("p s c -> p c s"), AX_X, ALU.max)
                        dve.drain()
                        dve.tensor_tensor(cmax[:], cmax[:], peak[h][:], ALU.max)
                        dve.drain()
                        dve.tensor_tensor(mdiff[:], peak[h][:], cmax[:], ALU.subtract).then_inc(s_md, 1)
                        dve.tensor_tensor(e2[h][:], e2[h][:], cmax[:].unsqueeze(1).broadcast_to([P, SLOT, CH]),
                                          ALU.subtract).then_inc(s_d, 1)
                        dve.drain()
                        dve.tensor_copy(peak[h][:], cmax[:])
                        rest_one(1 - h, g + 1 + h, g * 2 + h + 2)
                        scaled(e1, h, g * 8 + 4 * h + 3)
                        dve.drain().then_inc(s_nbr_free[h], 1)
                        rest_two(1 - h, g * 2 + h + 2)
                        if h == 0:
                            with dve.If(level > 0):
                                accumulate(1, g * 2 + 2)
                        else:
                            accumulate(0, g * 2 + 3)
                        dve.wait_ge(s_ex, g * 2 + h + 1)
                        dve.tensor_tensor(exm[h][:, :, CH:2 * CH], e1[:], exm[h][:, :, 0:CH], ALU.mult)
                        dve.drain().then_inc(s_p, 1)
                    dve.reg_add(step, step, 1)
                g = dve.snap(step, min_val=1, max_val=1 << 16)
                accumulate(1, g * 2 + 2)
                for h in range(2):
                    tile = bass.ds(q * 2 + h, 1)
                    dve.reciprocal(rden[:], acc[h][:, 0, :])
                    dve.drain()
                    dve.tensor_tensor(ratio[:], acc[h][:, 1, :], rden[:], ALU.mult)
                    dve.drain()
                    dve.tensor_reduce(ft[:], ratio[:].rearrange("p (i o) -> p o i", o=FEAT), AX_X, ALU.add)
                    dve.drain()
                    dve.tensor_scalar(ft[:], ft[:], has_edge[:, tile], None, ALU.mult)
                    dve.drain()
                    dve.tensor_tensor(x2[:, tile, :].rearrange("p a f -> p (a f)"), ft[:],
                                      x1[:, tile, :].rearrange("p a f -> p (a f)"), ALU.add)
                    dve.drain()
            layernorm(x2, 2)
            dve.drain().then_inc(s_x2, 1)


_INS = ['x', 'src', 'dst', 'edge_attr_16', 'L0_gnn_W1', 'L0_gnn_b1', 'L0_gnn_W2', 'L0_gnn_b2', 'L0_gnn_W3',
        'L0_gnn_b3', 'L1_gnn_W_msg', 'L1_gnn_b_msg', 'L1_gnn_W_attn', 'L1_gnn_b_attn']
_PADDED = {'x': (NP, 0), 'src': (EP, 0), 'dst': (NB * P, FAR), 'edge_attr_16': (EP, 0)}


def kernel(**inputs):
    import numpy as _np
    import concourse.bacc as _bacc
    from concourse import mybir as _mybir
    from concourse.bass_utils import run_bass_kernel_spmd as _run

    nc = _bacc.Bacc("TRN2", target_bir_lowering=False, num_devices=1)
    arrays, args = {}, []
    for name in _INS:
        a = _np.ascontiguousarray(inputs[name])
        if name in _PADDED:
            rows, value = _PADDED[name]
            full = _np.full((rows,) + a.shape[1:], value, a.dtype)
            full[:a.shape[0]] = a
            a = full
        arrays[f"in_{name}_dram"] = a
        args.append(nc.dram_tensor(f"in_{name}_dram", a.shape, _mybir.dt.from_np(a.dtype), kind="ExternalInput").ap())
    args.append(nc.dram_tensor("out_0_dram", (N, FEAT), F32, kind="ExternalOutput").ap())
    gnn_kernel(nc, *args)
    r = _run(nc, [arrays], core_ids=[0])
    return r.results[0]["out_0_dram"]
```

```python
from contextlib import ExitStack

import concourse.bass as bass
import numpy as np
from concourse import mybir

P = 128
F32 = mybir.dt.float32
BF16 = mybir.dt.bfloat16
F16 = mybir.dt.float16
I32 = mybir.dt.int32
I8 = mybir.dt.int8
ALU = mybir.AluOpType
ACT = mybir.ActivationFunctionType
AX_X = mybir.AxisListType.X
RMAX = bass.bass_isa.ReduceOp.max

N = 3125
E = 103125
FEAT = 16
HID = 64
CH = FEAT * FEAT
NG = -(-N // P)
NT = -(-(N + 1) // P)
NT += NT % 2
NP = NT * P
NPAIR = NT // 2
PAD = NG * P
NB = -(-E // P)
SLOT = 8
WIN = 512 // NG
NWIN = -(-N // WIN)
NWIN += NWIN % 2
DPAD = NWIN * WIN
DTAIL = NG * P - DPAD
DEPTH = 16
GROUP = 2
BASE = E * WIN // (N * P) + 1
BASE += -BASE % GROUP
EG = -(-(NB + DEPTH) // P)
EP = EG * P * P
FAR = 4096
CAP = 4000
TG = 5
TERMS = 6
KROWS = TERMS * FEAT + 4
MASKED = -1e30
EPS = 1e-5
MANY = 1 << 16


def gnn_kernel(nc, x, src, dst, edge_attr, W1, b1, W2, b2, W3, b3, W_msg, b_msg, W_attn, b_attn, out):
    rec_nat = nc.dram_tensor("node_records", [NP, 4], I32, kind="Internal").ap()
    rec_place = nc.dram_tensor("place_records", [NP, 4], I32, kind="Internal").ap()
    key_row = nc.dram_tensor("key_row", [NP], F32, kind="Internal").ap()
    win_rows = nc.dram_tensor("win_rows", [2, 2 * P], I32, kind="Internal").ap()
    table = nc.dram_tensor("table", [PAD + 1, FEAT], F32, kind="Internal").ap()
    ft_nat = nc.dram_tensor("ft_nat", [NP, FEAT], F32, kind="Internal").ap()

    with ExitStack() as ctx:
        def sb(name, shape, dt=F32, stack=ctx):
            return stack.enter_context(nc.sbuf_tensor(name, shape, dt))

        def sem(name):
            return ctx.enter_context(nc.semaphore(name))

        ident = sb("ident", [P, P])
        identb = sb("identb", [P, P], BF16)
        ones_row = sb("ones_row", [1, P])
        slot_no = sb("slot_no", [P, 2, SLOT])
        one_col = sb("one_col", [P, 1])
        eps_col = sb("eps_col", [P, 1])
        wk = sb("wk", [KROWS, 2 * CH], BF16)
        w1b = sb("w1b", [FEAT + 1, HID])
        w2 = sb("w2", [HID, HID])
        b2c = sb("b2c", [HID, 1])
        w3 = sb("w3", [HID, FEAT])
        b3r = sb("b3r", [P, FEAT])
        xn = sb("xn", [P, NG, FEAT])
        rec_n = sb("rec_n", [P, NG, 4], I32)
        dinv = sb("dinv", [P, NG])
        deg_n = sb("deg_n", [P, NG])
        has_edge = sb("has_edge", [P, NG])
        x1 = sb("x1", [P, NG, FEAT])
        stat = sb("stat", [P, NG])
        pad_row = sb("pad_row", [1, FEAT])
        rec_p = sb("rec_p", [P, NT, 4], I32)
        ids = sb("ids", [P, NT], I32)
        start_p = sb("start_p", [P, NT], I32)
        deg_p = sb("deg_p", [P, NT])
        deg_max = sb("deg_max", [P, NT])
        lev_f = sb("lev_f", [1, NPAIR])
        lev_i = sb("lev_i", [1, NPAIR], I32)
        levels = sb("levels", [1, NPAIR + 1], I32)
        lev_sum = sb("lev_sum", [1, 1])

        conv = ExitStack()
        counts = sb("counts", [P, NG * DPAD + DTAIL], F16, conv)
        edge_key = sb("edge_key", [P, EG * P], F32, conv)
        edge_low = sb("edge_low", [P, EG * P], BF16, conv)
        iota_key = sb("iota_key", [P, NG, WIN], F16, conv)
        iota_low = sb("iota_low", [P, P], BF16, conv)
        win_off = sb("win_off", [P, NWIN + 1], F32, conv)
        win_row_f = sb("win_row_f", [1, 2, NWIN], F32, conv)
        win_row_g = sb("win_row_g", [1, 2, NWIN], F32, conv)
        win_start = sb("win_start", [1, NWIN + 1], I32, conv)
        win_count = sb("win_count", [1, NWIN], I32, conv)
        planes = sb("planes", [1, 1], I32, conv)
        planes_f = sb("planes_f", [1, 1], F32, conv)
        plane_at = sb("plane_at", [1, 1], F32, conv)
        gfeat = sb("gfeat", [P, NG, HID], F32, conv)
        agg = sb("agg", [P, NG, HID], F32, conv)
        part = [sb(f"part{v}", [P, HID], F32, conv) for v in range(2)]
        node_f = sb("node_f", [P, NT + 1], F32, conv)
        node_m = sb("node_m", [P, NT + 1], F32, conv)
        blk_f = sb("blk_f", [P, NT + 1], F32, conv)
        blk_i = sb("blk_i", [P, NT + 1], I32, conv)
        below = sb("below", [P, NT + 1], F32, conv)
        rowptr = sb("rowptr", [P, NT + 1], F32, conv)
        deg_s = sb("deg_s", [P, NT], F32, conv)
        key = sb("key", [P, NT], F32, conv)
        key_neg = sb("key_neg", [P, NT], F32, conv)
        rank_f = sb("rank_f", [P, NT], F32, conv)
        rank_i = sb("rank_i", [P, NT], I32, conv)
        rec_s = sb("rec_s", [P, NT, 4], I32, conv)
        signs = gfeat[:].rearrange("p t f -> p (t f)").bitcast(I8)[:, 0:NP]
        hot = sb("hot", [P, (2 * GROUP + 1) * (NG * WIN + P)], BF16, conv)
        hot_key = hot[:, 0:(2 * GROUP + 1) * NG * WIN].rearrange("p (k n) -> p k n", n=NG * WIN)
        hot_low = hot[:, (2 * GROUP + 1) * NG * WIN:].rearrange("p (k n) -> p k n", n=P)
        near_key = [sb(f"near_key{v}", [P, DEPTH], F32, conv) for v in range(2)]
        near_low = [sb(f"near_low{v}", [P, DEPTH], BF16, conv) for v in range(2)]
        hT = hot[0:HID, 0:2 * TG * P].bitcast(F32)
        shared = sb("shared", [P, max(NP, NG * 3 * HID // 2 + TG * HID + TG * P)], F32, conv)
        dst_blk = shared[:, 0:NP].bitcast(I32).rearrange("p (t e) -> p t e", e=P)
        dst_blk_last = agg[:].rearrange("p t f -> p (t f)")[:, 0:P].bitcast(I32)
        key_all = shared[:, 0:NP]
        lo = NG * 3 * HID // 2
        gparts = shared[:, 0:lo].bitcast(BF16).rearrange("p (t f) -> p t f", t=NG)
        z = shared[:, lo:lo + TG * HID].rearrange("p (t f) -> p t f", t=TG)
        zT = shared[0:HID, lo + TG * HID:lo + TG * HID + TG * P]

        at = [0]

        def early(shape, dt=F32):
            size = 2 if dt in (F16, BF16) else 4
            words = size * int(np.prod(shape[1:])) // 2
            words += words % 2
            lo = at[0]
            at[0] += words
            v = counts[0:shape[0], lo:lo + size * int(np.prod(shape[1:])) // 2]
            if dt != F16:
                v = v.bitcast(dt)
            if len(shape) == 3:
                v = v.rearrange("p (a b) -> p a b", a=shape[1])
            return v

        dst_rows = early([P, EG, P], I32)
        src_rows_t = early([P, EG, P], I32)
        src_high = early([P, EG, P], I32)
        src_low = early([P, EG, P], I32)
        key_rows = early([P, EG, P])
        low_rows = early([P, EG, P])
        high_rows = early([P, EG, P])
        firsts_i = early([1, NB], I32)
        firsts_r = early([1, NB])
        firsts = early([P, NB])
        junk = early([P, NB])
        wf = early([FEAT, 2 * CH])
        wres = early([FEAT, 2 * CH])
        wsplit = early([FEAT, 3, 2 * CH], BF16)
        bf = early([1, 2 * CH])
        bres = early([1, 2 * CH])
        bsplit = early([1, 3, 2 * CH], BF16)
        mask_w = early([1, 2 * CH], BF16)
        node_i = early([P, NT + 1], I32)
        win_node_i = early([P, 4], I32)
        win_node = early([P, 4])
        win_blk = early([P, 4])
        win_blk_i = early([P, 4], I32)
        win_off_i = early([P, NWIN], I32)
        win_first = early([1, NWIN], I32)
        win_tiles = early([1, NWIN], I32)
        assert at[0] <= NG * DPAD
        conv.close()

        cursor = sb("cursor", [P, 2], I32)
        remain = sb("remain", [P, 2])
        src_run = [sb(f"src_run{h}", [P, SLOT], I32) for h in range(2)]
        src_rel = sb("src_rel", [P, 2, SLOT])
        used_slot = sb("used_slot", [P, 2, SLOT])
        slot_idx = sb("slot_idx", [P, 2 * SLOT], I32)
        nbr = [sb(f"nbr{h}", [P, SLOT * FEAT]) for h in range(2)]
        attr = [sb(f"attr{h}", [P, SLOT * FEAT]) for h in range(2)]
        hole = [sb(f"hole{h}", [P, SLOT]) for h in range(2)]
        terms = [sb(f"terms{h}", [P, SLOT, KROWS], BF16) for h in range(2)]
        res1 = sb("res1", [P, SLOT, FEAT])
        termsT = [sb(f"termsT{h}", [KROWS, SLOT * P], BF16) for h in range(2)]
        e2 = [sb(f"e2{h}", [P, SLOT, CH]) for h in range(2)]
        exm = [sb(f"exm{h}", [P, SLOT, 2 * CH]) for h in range(2)]
        e1 = sb("e1", [P, SLOT, CH])
        cmax = sb("cmax", [P, CH])
        peak = [sb(f"peak{h}", [P, CH]) for h in range(2)]
        mdiff = sb("mdiff", [P, CH])
        fade = [sb(f"fade{h}", [P, CH]) for h in range(2)]
        acc = [sb(f"acc{h}", [P, 2, CH]) for h in range(2)]
        rden = sb("rden", [P, CH])
        ratio = sb("ratio", [P, CH])
        ft_p = sb("ft_p", [P, NT, FEAT])
        x2 = sb("x2", [P, NG, FEAT])
        x2_sq = sb("x2_sq", [P, NG, FEAT])

        bank = [ctx.enter_context(nc.psum_tensor(f"bank{i}", [P, 512], F32)) for i in range(2)]
        pw = ctx.enter_context(nc.psum_tensor("pw", [P, 4, 512], F32))
        pt = ctx.enter_context(nc.psum_tensor("pt", [P, SLOT * P], BF16))
        psum_acc = ctx.enter_context(nc.psum_tensor("psum_acc", [P, 2 * CH], F32))
        flat = pw[:].rearrange("p b n -> p (b n)")

        s_edges = sem("s_edges")
        s_in = sem("s_in")
        s_wk = sem("s_wk")
        s_const = sem("s_const")
        s_frow = sem("s_frow")
        s_fbc = sem("s_fbc")
        s_blk = sem("s_blk")
        s_rows = sem("s_rows")
        s_turned = sem("s_turned")
        s_keys = sem("s_keys")
        s_win = sem("s_win")
        s_wind = sem("s_wind")
        s_winr = sem("s_winr")
        s_dblk = sem("s_dblk")
        s_below = sem("s_below")
        s_key = sem("s_key")
        s_keyd = sem("s_keyd")
        s_keyb = sem("s_keyb")
        s_natd = sem("s_natd")
        s_nat = sem("s_nat")
        s_rank = sem("s_rank")
        s_recd = sem("s_recd")
        s_recp = sem("s_recp")
        s_place = sem("s_place")
        s_dmax = sem("s_dmax")
        s_lev = sem("s_lev")
        s_deg = sem("s_deg")
        s_sqrt = sem("s_sqrt")
        s_wsp = sem("s_wsp")
        s_pads = sem("s_pads")
        s_padz = sem("s_padz")
        s_planes = sem("s_planes")
        s_hot = sem("s_hot")
        s_hot_free = sem("s_hot_free")
        s_tail = sem("s_tail")
        s_tail_free = sem("s_tail_free")
        s_near = sem("s_near")
        s_full = [sem(f"s_full{v}") for v in range(2)]
        s_full_free = [sem(f"s_full_free{v}") for v in range(2)]
        s_parts = sem("s_parts")
        s_counted = sem("s_counted")
        s_agg = [sem(f"s_agg{v}") for v in range(2)]
        s_agg_free = [sem(f"s_agg_free{v}") for v in range(2)]
        s_z = sem("s_z")
        s_zt = sem("s_zt")
        s_ztc = sem("s_ztc")
        s_ht = sem("s_ht")
        s_htc = sem("s_htc")
        s_mm = sem("s_mm")
        s_h = sem("s_h")
        s_x1 = sem("s_x1")
        s_tab = sem("s_tab")
        s_srun = sem("s_srun")
        s_settled = sem("s_settled")
        s_settled_pe = sem("s_settled_pe")
        s_settled_act = sem("s_settled_act")
        s_settled_dve = sem("s_settled_dve")
        s_nbr = [sem(f"s_nbr{h}") for h in range(2)]
        s_nbr_free = [sem(f"s_nbr_free{h}") for h in range(2)]
        s_attr = [sem(f"s_attr{h}") for h in range(2)]
        s_attr_free = [sem(f"s_attr_free{h}") for h in range(2)]
        s_hole = sem("s_hole")
        s_hi = sem("s_hi")
        s_mid = sem("s_mid")
        s_r1 = sem("s_r1")
        s_lo = sem("s_lo")
        s_tT = sem("s_tT")
        s_tTc = sem("s_tTc")
        s_w = sem("s_w")
        s_wfree = sem("s_wfree")
        s_d = sem("s_d")
        s_ex = sem("s_ex")
        s_md = sem("s_md")
        s_fade = sem("s_fade")
        s_p = sem("s_p")
        s_sum = sem("s_sum")
        s_accd = sem("s_accd")
        s_var = sem("s_var")
        s_std = sem("s_std")
        s_ft = sem("s_ft")
        s_ftn = sem("s_ftn")
        s_x2 = sem("s_x2")
        s_out = sem("s_out")
        s_final = sem("s_final")

        src_runs = src.rearrange("(e a) -> e a", a=1)
        dst_blocks = dst.rearrange("(b p) -> b p", p=P)

        def row(v):
            return v.rearrange("(a n) -> a n", a=1)

        block = ctx.enter_context(nc.Block())

        @block.sync
        def _(sp):
            sp.dma_start(firsts_i, dst_blocks[0:NB, 0:1].rearrange("b a -> a b"),
                         allow_slow_non_contiguous=True).then_inc(s_edges, 16)
            sp.dma_start(dst_rows, dst.rearrange("(g r p) -> r g p", r=P, p=P)).then_inc(s_edges, 16)
            sp.dma_start(src_rows_t, src.rearrange("(g r p) -> r g p", r=P, p=P)).then_inc(s_edges, 16)
            for to, what in ((w1b[0:FEAT, :], W1), (w1b[FEAT:FEAT + 1, :], row(b1)), (w2[:], W2),
                             (b2c[:], b2.rearrange("(n a) -> n a", a=1)), (w3[:], W3),
                             (b3r[:], row(b3).broadcast_to([P, FEAT])),
                             (xn[:], x[0:NG * P, :].rearrange("(t p) f -> p t f", p=P)),
                             (wf[:, 0:CH], W_attn), (wf[:, CH:2 * CH], W_msg),
                             (bf[:, 0:CH], row(b_attn)), (bf[:, CH:2 * CH], row(b_msg))):
                sp.dma_start(to, what).then_inc(s_in, 16)
            sp.wait_ge(s_win, 1)
            for k in range(2):
                sp.dma_start(win_rows[k].rearrange("(c p) -> p c", p=P), win_blk_i[:, 2 * k:2 * k + 2],
                             allow_slow_non_contiguous=True).then_inc(s_wind, 16)
            sp.wait_ge(s_wind, 32)
            sp.dma_start(win_first, win_rows[0:1, 0:NWIN]).then_inc(s_winr, 16)
            sp.dma_start(win_tiles, win_rows[1:2, 0:NWIN]).then_inc(s_winr, 16)
            sp.wait_ge(s_padz, 1)
            sp.dma_start(table[PAD:PAD + 1, :], pad_row[:]).then_inc(s_pads, 16)
            sp.wait_ge(s_wsp, 1)
            for t, k in enumerate((0, 1, 2, 0, 1, 0)):
                sp.dma_start(wk[t * FEAT:(t + 1) * FEAT, :], wsplit[:, k, :]).then_inc(s_wk, 16)
            for k in range(3):
                sp.dma_start(wk[TERMS * FEAT + k:TERMS * FEAT + k + 1, :], bsplit[:, k, :]).then_inc(s_wk, 16)
            sp.dma_start(wk[KROWS - 1:KROWS, :], mask_w).then_inc(s_wk, 16)
            sp.wait_ge(s_key, 1)
            sp.dma_start(key_row.rearrange("(p t) -> p t", p=P), key[:]).then_inc(s_keyd, 16)
            sp.dma_start(rec_nat.rearrange("(p t) c -> p t c", p=P), rec_s[:]).then_inc(s_natd, 16)
            sp.wait_ge(s_keyd, 16)
            sp.dma_start(key_all, row(key_row).broadcast_to([P, NP])).then_inc(s_keyb, 16)
            sp.wait_ge(s_natd, 16)
            sp.dma_start(rec_n[:], rec_nat[0:NG * P, :].rearrange("(t p) c -> p t c", p=P)).then_inc(s_nat, 16)
            sp.wait_ge(s_recd, 16 * NT)
            sp.dma_start(rec_p[:], rec_place.rearrange("(t p) c -> p t c", p=P)).then_inc(s_recp, 16)
            sp.wait_ge(s_x1, 1)
            sp.dma_start(table[0:NG * P, :].rearrange("(t p) f -> p t f", p=P), x1[:]).then_inc(s_tab, 16)
            sp.wait_ge(s_out, 16 * NT)
            sp.dma_start(x2[:], ft_nat[0:NG * P, :].rearrange("(t p) f -> p t f", p=P)).then_inc(s_ftn, 16)
            sp.wait_ge(s_x2, 1)
            whole = N // P
            sp.dma_start(out[0:whole * P, :].rearrange("(t p) f -> p t f", p=P), x2[:, 0:whole, :]).then_inc(s_final, 16)
            sp.dma_start(out[whole * P:N, :], x2[0:N - whole * P, whole, :]).then_inc(s_final, 16)
            sp.wait_ge(s_final, 32)

        @block.gpsimd
        def _(pool):
            pool.memset(ident[:], 0.0)
            pool.memset(identb[:], 0.0)
            pool.memset(ones_row[:], 1.0)
            pool.iota(node_i, pattern=[[1, NT + 1]], base=0, channel_multiplier=NT)
            for k in range(2):
                for c in range(2):
                    pool.iota(win_node_i[:, 2 * k + c:2 * k + c + 1], pattern=[[0, 1]],
                              base=(P * c + k) * WIN, channel_multiplier=WIN)
            pool.iota(win_off_i, pattern=[[-NG * WIN, NWIN]], base=0, channel_multiplier=0)
            pool.iota(iota_key[:], pattern=[[1, NG], [NG, WIN]], base=0, channel_multiplier=0,
                      allow_small_or_imprecise_dtypes=True)
            pool.iota(iota_low[:], pattern=[[1, P]], base=0, channel_multiplier=0,
                      allow_small_or_imprecise_dtypes=True)
            pool.iota(slot_no[:], pattern=[[0, 2], [1, SLOT]], base=0, channel_multiplier=0,
                      allow_small_or_imprecise_dtypes=True)
            pool.drain()
            for m in (ident, identb):
                pool.affine_select(out=m[:], in_=m[:], compare_op=ALU.not_equal, fill=1.0, base=0,
                                   pattern=[[-1, P]], channel_multiplier=1)
            pool.drain().then_inc(s_const, 1)
            pool.wait_ge(s_blk, 1)
            for t in range(NT + 1):
                to = dst_blk[:, t, :] if t < NT else dst_blk_last
                pool.indirect_dma_start(to, None, dst_blocks,
                                        bass.IndirectOffsetOnAxis(ap=blk_i[:, t:t + 1], axis=0)).then_inc(s_dblk, 16)
            pool.wait_ge(s_below, 1)
            pool.tensor_scalar(below[:], below[:], 0.5, P / 2.0, ALU.mult, ALU.add)
            pool.tensor_scalar(rowptr[:], blk_f[:], float(P), None, ALU.mult)
            pool.drain()
            pool.tensor_tensor(rowptr[:], rowptr[:], below[:], ALU.add)
            pool.drain()
            pool.tensor_tensor(deg_s[:], rowptr[:, 1:NT + 1], rowptr[:, 0:NT], ALU.subtract)
            pool.drain()
            pool.tensor_scalar(key[:], deg_s[:], float(CAP), 4096.0, ALU.min, ALU.mult)
            pool.drain()
            pool.tensor_tensor(key[:], key[:], node_f[:, 0:NT], ALU.subtract)
            pool.drain()
            pool.tensor_scalar(key[:], key[:], float(NP - 1), None, ALU.add)
            pool.drain()
            pool.tensor_scalar(key_neg[:], key[:], -1.0, None, ALU.mult)
            for c, v in enumerate((node_f[:, 0:NT], rowptr[:, 0:NT], deg_s[:], deg_s[:])):
                pool.tensor_copy(rec_s[:, :, c], v)
            pool.drain().then_inc(s_key, 1)
            pool.wait_ge(s_rank, 1)
            pool.tensor_scalar(rank_f[:], rank_f[:], NP - 1.0, 0.5, ALU.add, ALU.mult)
            pool.drain()
            pool.tensor_copy(rank_i[:], rank_f[:])
            pool.drain()
            for t in range(NT):
                pool.indirect_dma_start(rec_place, bass.IndirectOffsetOnAxis(ap=rank_i[:, t:t + 1], axis=0),
                                        rec_s[:, t, :], None).then_inc(s_recd, 16)
            pool.wait_ge(s_place, 1)
            pool.partition_all_reduce(deg_max[:], deg_p[:], P, RMAX).then_inc(s_dmax, 1)

            step = pool.alloc_register("pool_step")

            def wait(s, value):
                pool.wait_ge(s, value)
                pool.sem_inc(s_settled, 1)

            def run_gather(dst_tile, table_ap, h, signal):
                pool.indirect_dma_start(dst_tile[:], None, table_ap,
                                        bass.IndirectOffsetOnAxis(ap=cursor[:, h:h + 1], axis=0)).then_inc(signal, 16)

            def start_pair(q):
                pool.tensor_copy(cursor[:], start_p[:, bass.ds(q * 2, 2)])
                pool.tensor_copy(remain[:], deg_p[:, bass.ds(q * 2, 2)])
                pool.drain()

            def slot_indices(srun_signal, srun_value):
                pool.tensor_tensor(used_slot[:], remain[:].unsqueeze(2).broadcast_to([P, 2, SLOT]), slot_no[:],
                                   ALU.subtract)
                pool.drain()
                pool.tensor_scalar(used_slot[:], used_slot[:], 0.0, 1.0, ALU.max, ALU.min)
                wait(srun_signal, srun_value)
                for h in range(2):
                    pool.tensor_scalar(src_rel[:, h, :], src_run[h][:], float(PAD), None, ALU.subtract)
                pool.drain()
                pool.tensor_tensor(src_rel[:], src_rel[:], used_slot[:], ALU.mult)
                pool.drain()
                pool.tensor_scalar(slot_idx[:], src_rel[:].rearrange("p h s -> p (h s)"), float(PAD), None, ALU.add)
                pool.tensor_scalar(cursor[:], cursor[:], float(SLOT), float(E), ALU.add, ALU.min)
                pool.tensor_scalar(remain[:], remain[:], float(SLOT), None, ALU.subtract)

            def row_gathers(h, signal):
                for j in range(SLOT):
                    c = h * SLOT + j
                    pool.indirect_dma_start(nbr[h][:, j * FEAT:(j + 1) * FEAT], None, table,
                                            bass.IndirectOffsetOnAxis(ap=slot_idx[:, c:c + 1], axis=0)
                                            ).then_inc(signal, 16)

            pool.wait_ge(s_lev, 1)
            pool.wait_ge(s_pads, 16)
            pool.wait_ge(s_tab, 16)
            pool.reg_mov(step, 0)
            with pool.Fori(0, NPAIR) as q:
                n = pool.value_load(levels[0:1, bass.ds(q, 1)], min_val=1, max_val=E)
                start_pair(q)
                with pool.Fori(0, n) as _level:
                    g = pool.snap(step, min_val=0, max_val=MANY)
                    for h in range(2):
                        run_gather(src_run[h], src_runs, h, s_srun)
                    for h in range(2):
                        wait(s_attr_free[h], g + 1)
                        run_gather(attr[h], edge_attr, h, s_attr[h])
                    slot_indices(s_srun, g * 32 + 32)
                    for h in range(2):
                        pool.tensor_scalar(hole[h][:], used_slot[:, h, :], -1.0, 1.0, ALU.mult, ALU.add)
                    pool.drain().then_inc(s_hole, 1)
                    for h in range(2):
                        wait(s_nbr_free[h], g + 1)
                        row_gathers(h, s_nbr[h])
                    pool.reg_add(step, step, 1)
            g = pool.snap(step, min_val=0, max_val=MANY)
            wait(s_attr_free[0], g + 1)
            run_gather(attr[0], edge_attr, 0, s_attr[0])
            pool.nop().then_inc(s_hole, 1)
            pool.wait_ge(s_ft, 1)
            for t in range(NT):
                pool.indirect_dma_start(ft_nat, bass.IndirectOffsetOnAxis(ap=ids[:, t:t + 1], axis=0),
                                        ft_p[:, t, :], None).then_inc(s_out, 16)
            pool.wait_ge(s_out, 16 * NT)

        @block.tensor
        def _(pe):
            pe.wait_ge(s_const, 1)
            pe.wait_ge(s_frow, 1)
            half = NB // 2
            for i in range(2):
                mm = pe.matmul(bank[i][:, 0:half], ones_row[:], firsts_r[:, i * half:(i + 1) * half],
                               start=True, stop=True)
            mm.then_inc(s_fbc, 1)
            for k, v in enumerate((key_rows, low_rows)):
                pe.wait_ge(s_rows, k + 1)
                if k:
                    pe.wait_ge(s_keys, k)
                for g in range(EG):
                    mm = pe.transpose(flat[:, g * P:(g + 1) * P], v[:, g, :], ident[:])
                mm.then_inc(s_turned, 1)

            tile_no = pe.alloc_register("pe_tiles")
            wins = pe.alloc_register("pe_wins")
            fills = pe.alloc_register("pe_fills")
            group = pe.alloc_register("pe_group")
            late = pe.alloc_register("pe_late")
            for r in (tile_no, wins, fills, group, late):
                pe.reg_mov(r, 0)

            def count_plane():
                with pe.Fori(0, NWIN // 2) as i:
                    w = pe.snap(wins, min_val=0, max_val=MANY)
                    for v in range(2):
                        def count(k, first):
                            return pe.matmul(bank[v][:, 0:NG * WIN], hot_low[:, k, :], hot_key[:, k, :],
                                             start=first, stop=False, skip_group_check=True)

                        pe.wait_ge(s_full_free[v], w + 1)
                        pe.sem_inc(s_settled_pe, 1)
                        for a in range(BASE // GROUP):
                            at = v * (BASE // GROUP) + a
                            pe.wait_ge(s_hot, w * (2 * BASE // GROUP) + at + 1)
                            for k in range(GROUP):
                                mm = count(at % 2 * GROUP + k, a == 0 and k == 0)
                            mm.then_inc(s_hot_free, 1)
                        n = pe.value_load(win_count[0:1, bass.ds(i * 2 + v, 1)], min_val=1, max_val=DEPTH)
                        with pe.If(n > BASE):
                            with pe.Fori(BASE, n) as _k:
                                pe.wait_ge(s_tail, pe.snap(tile_no, min_val=0, max_val=MANY) + 1)
                                count(2 * GROUP, False).then_inc(s_tail_free, 1)
                                pe.reg_add(tile_no, tile_no, 1)
                        pe.drain().then_inc(s_full[v], 1)
                    pe.reg_add(wins, wins, 1)

            def sum_sources(f):
                def tile(t, v, g):
                    pe.wait_ge(s_agg_free[v], g + 1)
                    for a in range(NG):
                        mm = pe.matmul(pw[:, v, 0:3 * f], counts[:, bass.ds(t * P + a * DPAD, P)],
                                       gparts[:, a, 0:3 * f], start=(a == 0), stop=(a == NG - 1))
                    mm.then_inc(s_agg[v], 1)

                with pe.Fori(0, NG // 2) as i:
                    g = pe.snap(fills, min_val=0, max_val=MANY)
                    for v in range(2):
                        tile(i * 2 + v, v, g)
                    pe.reg_add(fills, fills, 1)
                g = pe.snap(fills, min_val=0, max_val=MANY)
                tile(NG - 1, 0, g)
                pe.wait_ge(s_agg_free[1], g + 1)
                pe.sem_inc(s_settled_pe, 1)
                pe.nop().then_inc(s_agg[1], 1)
                pe.reg_add(fills, fills, 1)

            def weights(layer):
                f = (FEAT, HID)[layer]
                with pe.Fori(0, NG // TG) as _i:
                    g = pe.snap(group, min_val=0, max_val=MANY)
                    pe.wait_ge(s_z, g + 1)
                    pe.sem_inc(s_settled_pe, 1)
                    for t in range(TG):
                        mm = pe.transpose(flat[0:f, t * P:(t + 1) * P], z[:, t, 0:f], ident[:])
                    mm.then_inc(s_zt, 1)
                    pe.wait_ge(s_ztc, g + 1)
                    pe.sem_inc(s_settled_pe, 1)
                    if layer == 0:
                        for t in range(TG):
                            mm = pe.matmul(bank[0][:, t * HID:(t + 1) * HID], zT[0:FEAT + 1, t * P:(t + 1) * P],
                                           w1b[:], start=True, stop=True)
                    else:
                        pe.matmul(flat[0:HID, 1024:1536], w2[:], zT[:, 0:512], start=True, stop=True)
                        pe.matmul(flat[0:HID, 1536:1536 + TG * P - 512], w2[:], zT[:, 512:TG * P],
                                  start=True, stop=True).then_inc(s_ht, 1)
                        pe.wait_ge(s_htc, pe.snap(late, min_val=0, max_val=MANY) + 1)
                        pe.sem_inc(s_settled_pe, 1)
                        for t in range(TG):
                            mm = pe.matmul(bank[0][:, t * FEAT:(t + 1) * FEAT], hT[:, t * P:(t + 1) * P], w3[:],
                                           start=True, stop=True)
                        pe.reg_add(late, late, 1)
                    mm.then_inc(s_mm, 1)
                    pe.reg_add(group, group, 1)

            pe.wait_ge(s_in, 16 * 11)
            plane = pe.alloc_register("pe_plane")
            pe.reg_mov(plane, 0)
            for layer in range(3):
                if layer == 0:
                    pe.wait_ge(s_planes, 1)
                    np_ = pe.value_load(planes[0:1, 0:1], min_val=1, max_val=64)
                with pe.Fori(0, np_) as _p:
                    c = pe.snap(plane, min_val=0, max_val=MANY)
                    pe.wait_ge(s_planes, c + 1)
                    pe.sem_inc(s_settled_pe, 1)
                    if layer == 0:
                        count_plane()
                    else:
                        with pe.If(np_ > 1):
                            count_plane()
                    pe.wait_ge(s_parts, c + 1)
                    pe.sem_inc(s_settled_pe, 1)
                    sum_sources((FEAT, HID, FEAT)[layer])
                    pe.reg_add(plane, plane, 1)
                if layer < 2:
                    weights(layer)

            step = pe.alloc_register("pe_step")

            def turn(h, v):
                pe.wait_ge(s_lo, v)
                pe.wait_ge(s_tTc, v)
                for j in range(SLOT):
                    mm = pe.transpose(pt[0:KROWS, j * P:(j + 1) * P], terms[h][:, j, :], identb[:])
                mm.then_inc(s_tT, 1)

            def product(h, m, value):
                for i in range(2):
                    pe.wait_ge(s_wfree, value + i)
                    for j in range(4 * i, 4 * i + 4):
                        mm = pe.matmul(pw[:, 2 * i + j % 4 // 2, (j % 2) * CH:(j % 2 + 1) * CH],
                                       termsT[h][:, j * P:(j + 1) * P], wk[:, m * CH:(m + 1) * CH],
                                       start=True, stop=True)
                    mm.then_inc(s_w, 1)

            def sums(h, v):
                pe.wait_ge(s_p, v)
                pe.wait_ge(s_accd, v)
                for j in range(SLOT):
                    mm = pe.matmul(psum_acc[:], ident[:], exm[h][:, j, :], start=(j == 0), stop=(j == SLOT - 1))
                mm.then_inc(s_sum, 1)

            pe.wait_ge(s_wk, 16 * (TERMS + 4))
            pe.wait_ge(s_lev, 1)
            pe.reg_mov(step, 0)
            turn(0, 1)
            pe.wait_ge(s_tTc, 2)
            product(0, 0, 1)
            total = pe.value_load(levels[0:1, NPAIR:NPAIR + 1], min_val=1, max_val=MANY)
            with pe.Fori(0, total) as _s:
                g = pe.snap(step, min_val=0, max_val=MANY)
                for h in range(2):
                    product(h, 1, g * 8 + 4 * h + 3)
                    turn(1 - h, g * 2 + h + 2)
                    pe.wait_ge(s_tTc, g * 2 + h + 3)
                    product(1 - h, 0, g * 8 + 4 * h + 5)
                    sums(h, g * 2 + h + 1)
                pe.reg_add(step, step, 1)

        @block.scalar
        def _(act):
            for k, to in enumerate((edge_key, edge_low)):
                act.wait_ge(s_turned, k + 1)
                act.copy(to[:], flat[:, 0:EG * P]).then_inc(s_keys, 1)

            def count_below():
                act.wait_ge(s_dblk, 16 * (NT + 1))
                for t in range(NT + 1):
                    block_t = dst_blk[:, t, :] if t < NT else dst_blk_last
                    act.activation(signs[:, t * P % NP:t * P % NP + P], block_t, ACT.Sign, bias=node_m[:, t:t + 1],
                                   scale=-1.0, accum_out=below[:, t:t + 1])
                    if t == NT - 1:
                        act.drain()
                act.drain().then_inc(s_below, 1)

            wins = act.alloc_register("act_wins")
            group = act.alloc_register("act_group")
            late = act.alloc_register("act_late")
            for r in (wins, group, late):
                act.reg_mov(r, 0)

            def keep_counts(lo, hi):
                with act.Fori(lo, hi) as i:
                    w = act.snap(wins, min_val=0, max_val=MANY)
                    for v in range(2):
                        act.wait_ge(s_full[v], w + 1)
                        act.copy(counts[:, 0:NG * DPAD].rearrange("p (a d) -> p a d", a=NG)
                                 [:, :, bass.ds(i * 2 * WIN + v * WIN, WIN)],
                                 bank[v][:, 0:NG * WIN].rearrange("p (a d) -> p a d", a=NG)
                                 ).then_inc(s_full_free[v], 1)
                    act.reg_add(wins, wins, 1)

            plane = act.alloc_register("act_plane")
            act.reg_mov(plane, 0)
            early_windows = NWIN // 8
            assert early_windows + 2 * NT < NWIN // 2
            for layer in range(3):
                if layer == 0:
                    act.wait_ge(s_planes, 1)
                    np_ = act.value_load(planes[0:1, 0:1], min_val=1, max_val=64)
                with act.Fori(0, np_) as _p:
                    c = act.snap(plane, min_val=0, max_val=MANY)
                    act.wait_ge(s_planes, c + 1)
                    act.sem_inc(s_settled_act, 1)
                    if layer == 0:
                        keep_counts(0, early_windows)
                        with act.If(c < 1):
                            count_below()
                        with act.Fori(0, NT) as t:
                            with act.If(c < 1):
                                act.wait_ge(s_keyb, 16)
                                act.activation(signs, key_all, ACT.Sign, bias=key_neg[:, bass.ds(t, 1)],
                                               accum_out=rank_f[:, bass.ds(t, 1)])
                                act.drain()
                            keep_counts(t * 2 + early_windows, t * 2 + early_windows + 2)
                        act.drain().then_inc(s_rank, 1)
                        keep_counts(early_windows + 2 * NT, NWIN // 2)
                    else:
                        with act.If(np_ > 1):
                            keep_counts(0, NWIN // 2)
                    act.drain().then_inc(s_counted, 1)
                    act.reg_add(plane, plane, 1)
                if layer == 0:
                    act.wait_ge(s_deg, 1)
                    act.activation(dinv[:], deg_n[:], ACT.Sqrt, bias=one_col[:]).then_inc(s_sqrt, 1)
                if layer < 2:
                    f = (FEAT, HID)[layer]
                    with act.Fori(0, NG // TG) as _i:
                        g = act.snap(group, min_val=0, max_val=MANY)
                        act.wait_ge(s_zt, g + 1)
                        act.copy(zT[0:f, :], flat[0:f, 0:TG * P]).then_inc(s_ztc, 1)
                        if layer == 1:
                            act.wait_ge(s_ht, act.snap(late, min_val=0, max_val=MANY) + 1)
                            act.activation(hT, flat[0:HID, 1024:1024 + TG * P], ACT.Relu, bias=b2c[:]
                                           ).then_inc(s_htc, 1)
                            act.reg_add(late, late, 1)
                        act.reg_add(group, group, 1)
            act.wait_ge(s_var, 1)
            act.activation(stat[:], stat[:], ACT.Sqrt, bias=eps_col[:]).then_inc(s_std, 1)
            step = act.alloc_register("act_step")

            def high(h, value):
                act.wait_ge(s_attr[h], value)
                act.copy(terms[h][:, :, 0:3 * FEAT].rearrange("p s (t f) -> p s t f", t=3),
                         attr[h][:].rearrange("p (s f) -> p s f", s=SLOT).unsqueeze(2)
                         .broadcast_to([P, SLOT, 3, FEAT])).then_inc(s_hi, 1)

            def middle(h, v):
                act.wait_ge(s_r1, v)
                act.copy(terms[h][:, :, 3 * FEAT:5 * FEAT].rearrange("p s (t f) -> p s t f", t=2),
                         res1[:].unsqueeze(2).broadcast_to([P, SLOT, 2, FEAT])).then_inc(s_mid, 1)

            def turned(h, v):
                act.wait_ge(s_tT, v)
                act.copy(termsT[h][:], pt[0:KROWS, :]).then_inc(s_tTc, 1)

            act.sem_inc(s_tTc, 1)
            act.wait_ge(s_lev, 1)
            act.reg_mov(step, 0)
            high(0, 16)
            middle(0, 1)
            turned(0, 1)
            total = act.value_load(levels[0:1, NPAIR:NPAIR + 1], min_val=1, max_val=MANY)
            with act.Fori(0, total) as _s:
                g = act.snap(step, min_val=0, max_val=MANY)
                for h in range(2):
                    high(1 - h, g * 16 + 16 + 16 * h)
                    act.wait_ge(s_md, g * 2 + h + 1)
                    act.activation(fade[h][:], mdiff[:], ACT.Exp).then_inc(s_fade, 1)
                    act.wait_ge(s_d, g * 2 + h + 1)
                    act.wait_ge(s_sum, g * 2 + h + 1)
                    act.activation(exm[h][:, :, 0:CH], e2[h][:], ACT.Exp).then_inc(s_ex, 1)
                    middle(1 - h, g * 2 + h + 2)
                    turned(1 - h, g * 2 + h + 2)
                act.reg_add(step, step, 1)
            act.wait_ge(s_var, 2)
            act.activation(stat[:], stat[:], ACT.Sqrt, bias=eps_col[:]).then_inc(s_std, 1)

        @block.vector
        def _(dve):
            dve.memset(pad_row[:], 1.0).then_inc(s_padz, 1)
            dve.memset(one_col[:], 1.0)
            dve.memset(eps_col[:], EPS)
            dve.memset(mask_w[:, 0:CH], MASKED)
            dve.memset(mask_w[:, CH:2 * CH], 0.0)
            dve.memset(counts[:, NG * DPAD:NG * DPAD + DTAIL], 0.0)
            dve.memset(plane_at[:], 0.0)
            dve.memset(win_start[:, NWIN:NWIN + 1], 0)
            dve.memset(win_off[:, NWIN:NWIN + 1], 0.0)
            for s in (s_tail_free, s_near, *s_full_free, *s_agg_free, *s_attr_free, *s_nbr_free, s_accd):
                dve.sem_inc(s, 1)
            for s in (s_wfree, s_sum):
                dve.sem_inc(s, 2)
            dve.sem_inc(s_hot_free, 2)

            dve.wait_ge(s_edges, 48)
            dve.tensor_copy(firsts_r, firsts_i).then_inc(s_frow, 1)
            dve.wait_ge(s_const, 1)
            dve.tensor_copy(win_node, win_node_i)
            dve.tensor_copy(win_off[:, 0:NWIN], win_off_i)
            dve.tensor_copy(node_f[:], node_i)
            dve.drain()
            dve.tensor_scalar(node_m[:], node_f[:], -0.5, None, ALU.add)
            dve.wait_ge(s_fbc, 1)
            half = NB // 2
            for i in range(2):
                dve.tensor_copy(firsts[:, i * half:(i + 1) * half], bank[i][:, 0:half])
            dve.drain()
            for k in range(4):
                dve.tensor_scalar(junk, firsts, win_node[:, k:k + 1], 0.0, ALU.is_lt, ALU.add,
                                  accum_out=win_blk[:, k:k + 1])
                dve.drain()
            dve.tensor_scalar(win_blk[:, 0:2], win_blk[:, 0:2], -1.0, 0.0, ALU.add, ALU.max)
            dve.drain()
            dve.tensor_tensor(win_blk[:, 2:4], win_blk[:, 2:4], win_blk[:, 0:2], ALU.subtract)
            dve.drain()
            dve.tensor_copy(win_blk_i, win_blk).then_inc(s_win, 1)
            for t in range(NT + 1):
                dve.tensor_scalar(junk, firsts, node_f[:, t:t + 1], 0.0, ALU.is_lt, ALU.add,
                                  accum_out=blk_f[:, t:t + 1])
                dve.drain()
            dve.tensor_scalar(blk_f[:], blk_f[:], -1.0, 0.0, ALU.add, ALU.max)
            dve.drain()
            dve.tensor_copy(blk_i[:], blk_f[:]).then_inc(s_blk, 1)
            dve.tensor_scalar(src_high, src_rows_t, P.bit_length() - 1, None, ALU.logical_shift_right)
            dve.tensor_scalar(src_low, src_rows_t, P - 1, None, ALU.bitwise_and)
            dve.drain()
            dve.tensor_copy(high_rows, src_high)
            dve.drain()
            dve.scalar_tensor_tensor(out=key_rows, in0=dst_rows, scalar=float(NG), in1=high_rows,
                                     op0=ALU.mult, op1=ALU.add).then_inc(s_rows, 1)
            dve.tensor_copy(low_rows, src_low).then_inc(s_rows, 1)
            dve.wait_ge(s_in, 16 * 11)
            for full, rest_, part3 in ((wf, wres, wsplit), (bf, bres, bsplit)):
                dve.tensor_copy(part3[:, 0, :], full)
                dve.drain()
                dve.tensor_tensor(rest_, full, part3[:, 0, :], ALU.subtract)
                dve.drain()
                dve.tensor_copy(part3[:, 1, :], rest_)
                dve.drain()
                dve.tensor_tensor(part3[:, 2, :], rest_, part3[:, 1, :], ALU.subtract)
            dve.drain().then_inc(s_wsp, 1)

            dve.wait_ge(s_wk, 16 * (TERMS + 4))
            dve.wait_ge(s_winr, 32)
            dve.tensor_copy(win_row_f[:, 0, :], win_first)
            dve.tensor_copy(win_row_f[:, 1, :], win_tiles)
            dve.drain()
            dve.tensor_reduce(planes_f[:], win_row_f[:, 1, :], AX_X, ALU.max)
            dve.drain()
            dve.tensor_scalar(planes_f[:], planes_f[:], DEPTH - 1.0, float(DEPTH), ALU.add, ALU.max)
            dve.drain()
            dve.tensor_copy(planes[:], planes_f[:])
            dve.drain()
            dve.tensor_scalar(planes[:], planes[:], DEPTH.bit_length() - 1, None, ALU.logical_shift_right)
            dve.drain()
            np_ = dve.value_load(planes[0:1, 0:1], min_val=1, max_val=64)

            tile_no = dve.alloc_register("dve_tiles")
            windows = dve.alloc_register("dve_windows")
            fills = dve.alloc_register("dve_fills")
            group = dve.alloc_register("dve_group")
            for r in (tile_no, windows, fills, group):
                dve.reg_mov(r, 0)

            def plane_tables():
                dve.tensor_scalar(win_row_g[:, 0, :], win_row_f[:, 0, :], plane_at[:], float(NB), ALU.add, ALU.min)
                dve.tensor_scalar(win_row_g[:, 1, :], win_row_f[:, 1, :], plane_at[:], float(DEPTH),
                                  ALU.subtract, ALU.min)
                dve.drain()
                dve.tensor_scalar(win_row_g[:, 1, :], win_row_g[:, 1, :], 1.0, None, ALU.max)
                dve.tensor_scalar(plane_at[:], plane_at[:], float(DEPTH), None, ALU.add)
                dve.drain()
                dve.tensor_copy(win_start[:, 0:NWIN], win_row_g[:, 0, :])
                dve.tensor_copy(win_count[:], win_row_g[:, 1, :])
                dve.drain().then_inc(s_planes, 1)

            def near(window, v):
                t0 = dve.value_load(win_start[0:1, bass.ds(window, 1)], min_val=0, max_val=NB)
                dve.tensor_scalar(near_key[v][:], edge_key[:, bass.ds(t0, DEPTH)], win_off[:, bass.ds(window, 1)],
                                  None, ALU.add)
                return dve.tensor_copy(near_low[v][:], edge_low[:, bass.ds(t0, DEPTH)])

            def one_hot(slot, v, k):
                dve.tensor_scalar(hot_key[:, slot, :].rearrange("p (a d) -> p a d", a=NG), iota_key[:],
                                  near_key[v][:, k], None, ALU.is_equal)
                return dve.tensor_scalar(hot_low[:, slot, :], iota_low[:], near_low[v][:, k], None, ALU.is_equal)

            def one_hot_plane():
                near(0, 0)
                dve.drain()
                with dve.Fori(0, NWIN // 2) as i:
                    w = dve.snap(windows, min_val=0, max_val=MANY)
                    for v in range(2):
                        dve.wait_ge(s_near, w * 2 + v + 1)
                        for a in range(BASE // GROUP):
                            at = v * (BASE // GROUP) + a
                            dve.wait_ge(s_hot_free, w * (2 * BASE // GROUP) + at + 1)
                            for k in range(GROUP):
                                hot_row = one_hot(at % 2 * GROUP + k, v, slice(a * GROUP + k, a * GROUP + k + 1))
                            hot_row.then_inc(s_hot, 1)
                            if a == 1:
                                dve.wait_ge(s_hot, w * (2 * BASE // GROUP) + at)
                                near(i * 2 + v + 1, 1 - v).then_inc(s_near, 1)
                        n = dve.value_load(win_count[0:1, bass.ds(i * 2 + v, 1)], min_val=1, max_val=DEPTH)
                        with dve.If(n > BASE):
                            with dve.Fori(BASE, n) as k:
                                dve.wait_ge(s_tail_free, dve.snap(tile_no, min_val=0, max_val=MANY) + 1)
                                one_hot(2 * GROUP, v, bass.ds(k, 1)).then_inc(s_tail, 1)
                                dve.reg_add(tile_no, tile_no, 1)
                    dve.reg_add(windows, windows, 1)

            def take_sums(f):
                def tile(t, v, g):
                    dve.wait_ge(s_agg[v], g + 1)
                    dve.tensor_reduce(part[v][:, 0:f], pw[:, v, 0:3 * f].rearrange("p (k f) -> p f k", k=3), AX_X,
                                      ALU.add).then_inc(s_agg_free[v], 1)
                    dve.drain()
                    here = agg[:, bass.ds(t, 1), 0:f]
                    dve.tensor_tensor(here, here, part[v][:, 0:f].unsqueeze(1), ALU.add)
                    dve.drain()

                with dve.Fori(0, NG // 2) as i:
                    g = dve.snap(fills, min_val=0, max_val=MANY)
                    for v in range(2):
                        tile(i * 2 + v, v, g)
                    dve.reg_add(fills, fills, 1)
                g = dve.snap(fills, min_val=0, max_val=MANY)
                tile(NG - 1, 0, g)
                dve.wait_ge(s_agg[1], g + 1)
                dve.nop().then_inc(s_agg_free[1], 1)
                dve.reg_add(fills, fills, 1)

            def split_features(f):
                for k in range(3):
                    to = gparts[:, :, k * f:(k + 1) * f]
                    full = gfeat[:, :, 0:f] if k == 0 else agg[:, :, 0:f]
                    if k < 2:
                        dve.tensor_copy(to, full)
                        dve.drain()
                        dve.tensor_tensor(agg[:, :, 0:f], full, to, ALU.subtract)
                        dve.drain()
                    else:
                        dve.tensor_copy(to, full)
                        dve.drain()
                dve.memset(agg[:], 0.0)
                dve.drain()

            def place_nodes():
                dve.wait_ge(s_recp, 16)
                dve.tensor_copy(ids[:], rec_p[:, :, 0])
                dve.tensor_copy(start_p[:], rec_p[:, :, 1])
                dve.tensor_copy(deg_p[:], rec_p[:, :, 2])
                dve.drain().then_inc(s_place, 1)
                dve.wait_ge(s_dmax, 1)
                dm = deg_max[0:1, :].rearrange("a (q h) -> a q h", h=2)
                dve.tensor_tensor(lev_f[:], dm[:, :, 0], dm[:, :, 1], ALU.max)
                dve.drain()
                dve.tensor_scalar(lev_f[:], lev_f[:], float(SLOT - 1), float(SLOT), ALU.add, ALU.max)
                dve.drain()
                dve.tensor_copy(lev_i[:], lev_f[:])
                dve.drain()
                dve.tensor_scalar(levels[:, 0:NPAIR], lev_i[:], SLOT.bit_length() - 1, None, ALU.logical_shift_right)
                dve.drain()
                dve.tensor_copy(lev_f[:], levels[:, 0:NPAIR])
                dve.drain()
                dve.tensor_reduce(lev_sum[:], lev_f[:], AX_X, ALU.add)
                dve.drain()
                dve.tensor_copy(levels[:, NPAIR:NPAIR + 1], lev_sum[:])

            dinv_wide = dinv[:].unsqueeze(2).broadcast_to([P, NG, FEAT])
            plane = dve.alloc_register("dve_plane")
            dve.reg_mov(plane, 0)
            dve.wait_ge(s_keys, 2)
            for layer in range(3):
                f = (FEAT, HID, FEAT)[layer]
                if layer:
                    split_features(f)
                if layer == 2:
                    place_nodes()
                with dve.Fori(0, np_) as _p:
                    c = dve.snap(plane, min_val=0, max_val=MANY)
                    plane_tables()
                    if layer == 0:
                        one_hot_plane()
                        with dve.If(c < 1):
                            dve.wait_ge(s_rank, 1)
                            dve.memset(zT, 1.0)
                            dve.wait_ge(s_nat, 16)
                            dve.tensor_copy(deg_n[:], rec_n[:, :, 2])
                            dve.drain().then_inc(s_deg, 1)
                            dve.wait_ge(s_sqrt, 1)
                            dve.reciprocal(dinv[:], dinv[:])
                            dve.drain()
                            dve.tensor_tensor(gfeat[:, :, 0:FEAT], xn[:], dinv_wide, ALU.mult)
                            dve.tensor_scalar(has_edge[:], deg_n[:], 1.0, None, ALU.min)
                            dve.drain()
                            split_features(FEAT)
                    else:
                        with dve.If(np_ > 1):
                            one_hot_plane()
                    dve.wait_ge(s_counted, c + 1)
                    dve.sem_inc(s_settled_dve, 1)
                    dve.drain().then_inc(s_parts, 1)
                    take_sums(f)
                    dve.reg_add(plane, plane, 1)
                dve.tensor_scalar(plane_at[:], plane_at[:], 0.0, None, ALU.mult)
                dve.drain()
                if layer < 2:
                    with dve.Fori(0, NG // TG) as i:
                        g = dve.snap(group, min_val=0, max_val=MANY)
                        tiles = bass.ds(i * TG, TG)
                        scale = dinv[:, tiles].unsqueeze(2)
                        dve.tensor_tensor(z[:, :, 0:f], agg[:, tiles, 0:f], gfeat[:, tiles, 0:f], ALU.add)
                        dve.drain()
                        dve.tensor_tensor(z[:, :, 0:f], z[:, :, 0:f], scale.broadcast_to([P, TG, f]),
                                          ALU.mult).then_inc(s_z, 1)
                        dve.wait_ge(s_mm, g + 1)
                        if layer == 0:
                            res = bank[0][:, 0:TG * HID].rearrange("p (t f) -> p t f", t=TG)
                            new = gfeat[:, tiles, :]
                            dve.tensor_tensor(new, res, scale.broadcast_to([P, TG, HID]), ALU.mult)
                            dve.drain()
                            dve.tensor_scalar(new, new, 0.0, None, ALU.max)
                        else:
                            res = bank[0][:, 0:TG * FEAT].rearrange("p (t f) -> p t f", t=TG)
                            dve.tensor_tensor(gfeat[:, tiles, 0:FEAT], res, scale.broadcast_to([P, TG, FEAT]),
                                              ALU.mult)
                        dve.drain()
                        dve.reg_add(group, group, 1)
            wide = [P, NG, FEAT]
            dve.tensor_tensor(x1[:], agg[:, :, 0:FEAT], gfeat[:, :, 0:FEAT], ALU.add)
            dve.drain()
            dve.tensor_tensor(x1[:], x1[:], dinv_wide, ALU.mult)
            dve.drain()
            dve.tensor_tensor(x1[:], x1[:], b3r[:].unsqueeze(1).broadcast_to(wide), ALU.add)
            dve.drain()
            dve.tensor_tensor(x1[:], x1[:], xn[:], ALU.add)

            def layernorm(v, squares, count):
                dve.drain()
                dve.tensor_reduce(stat[:], v[:], AX_X, ALU.add)
                dve.drain()
                dve.tensor_scalar(stat[:], stat[:], 1.0 / FEAT, None, ALU.mult)
                dve.drain()
                dve.tensor_tensor(v[:], v[:], stat[:].unsqueeze(2).broadcast_to(wide), ALU.subtract)
                dve.drain()
                dve.tensor_tensor(squares, v[:], v[:], ALU.mult)
                dve.drain()
                dve.tensor_reduce(stat[:], squares, AX_X, ALU.add)
                dve.drain()
                dve.tensor_scalar(stat[:], stat[:], 1.0 / FEAT, None, ALU.mult).then_inc(s_var, 1)
                dve.wait_ge(s_std, count)
                dve.reciprocal(stat[:], stat[:])
                dve.drain()
                dve.tensor_tensor(v[:], v[:], stat[:].unsqueeze(2).broadcast_to(wide), ALU.mult)

            layernorm(x1, agg[:, :, FEAT:2 * FEAT], 1)
            dve.drain().then_inc(s_x1, 1)

            for h in range(2):
                dve.memset(terms[h][:, :, TERMS * FEAT:KROWS], 1.0)
            dve.drain().then_inc(s_lev, 1)
            step = dve.alloc_register("dve_step")

            def rest_one(h, hole_value, v):
                dve.wait_ge(s_hole, hole_value)
                dve.wait_ge(s_hi, v)
                dve.tensor_copy(terms[h][:, :, KROWS - 1:KROWS].rearrange("p s a -> p (s a)"), hole[h][:])
                dve.tensor_tensor(res1[:], attr[h][:].rearrange("p (s f) -> p s f", s=SLOT),
                                  terms[h][:, :, 0:FEAT], ALU.subtract).then_inc(s_r1, 1)
                dve.drain().then_inc(s_attr_free[h], 1)

            def rest_two(h, v):
                dve.wait_ge(s_mid, v)
                dve.tensor_tensor(terms[h][:, :, 5 * FEAT:6 * FEAT], res1[:], terms[h][:, :, 3 * FEAT:4 * FEAT],
                                  ALU.subtract)
                dve.drain().then_inc(s_lo, 1)

            def scaled(to, h, value):
                for i in range(2):
                    dve.wait_ge(s_w, value + i)
                    h_src = nbr[h][:, 4 * i * FEAT:(4 * i + 4) * FEAT].unsqueeze(2)
                    dve.tensor_tensor(to[:, 4 * i:4 * i + 4, :].rearrange("p s (i o) -> p (s i) o", o=FEAT),
                                      pw[:, 2 * i:2 * i + 2, :].rearrange("p b (s i o) -> p (b s i) o", s=2, o=FEAT),
                                      h_src.broadcast_to([P, 4 * FEAT, FEAT]), ALU.mult).then_inc(s_wfree, 1)

            def accumulate(h, v):
                dve.wait_ge(s_sum, v)
                dve.tensor_tensor(acc[h][:], acc[h][:], fade[h][:].unsqueeze(1).broadcast_to([P, 2, CH]), ALU.mult)
                dve.drain()
                dve.tensor_tensor(acc[h][:].rearrange("p a c -> p (a c)"), acc[h][:].rearrange("p a c -> p (a c)"),
                                  psum_acc[:], ALU.add)
                dve.drain().then_inc(s_accd, 1)

            dve.reg_mov(step, 0)
            rest_one(0, 1, 1)
            rest_two(0, 1)
            with dve.Fori(0, NPAIR) as q:
                n = dve.value_load(levels[0:1, bass.ds(q, 1)], min_val=1, max_val=E)
                for h in range(2):
                    dve.memset(peak[h][:], -3e38)
                    dve.memset(acc[h][:], 0.0)
                dve.drain()
                with dve.Fori(0, n) as level:
                    g = dve.snap(step, min_val=0, max_val=MANY)
                    for h in range(2):
                        dve.wait_ge(s_nbr[h], g * 16 * SLOT + 16 * SLOT)
                        scaled(e2[h], h, g * 8 + 4 * h + 1)
                        dve.drain()
                        dve.tensor_reduce(cmax[:], e2[h][:].rearrange("p s c -> p c s"), AX_X, ALU.max)
                        dve.drain()
                        dve.tensor_tensor(cmax[:], cmax[:], peak[h][:], ALU.max)
                        dve.drain()
                        dve.tensor_tensor(mdiff[:], peak[h][:], cmax[:], ALU.subtract).then_inc(s_md, 1)
                        dve.tensor_tensor(e2[h][:], e2[h][:], cmax[:].unsqueeze(1).broadcast_to([P, SLOT, CH]),
                                          ALU.subtract).then_inc(s_d, 1)
                        dve.drain()
                        dve.tensor_copy(peak[h][:], cmax[:])
                        rest_one(1 - h, g + 1 + h, g * 2 + h + 2)
                        scaled(e1, h, g * 8 + 4 * h + 3)
                        dve.drain().then_inc(s_nbr_free[h], 1)
                        rest_two(1 - h, g * 2 + h + 2)
                        if h == 0:
                            with dve.If(level > 0):
                                accumulate(1, g * 2 + 2)
                        else:
                            accumulate(0, g * 2 + 3)
                        dve.wait_ge(s_ex, g * 2 + h + 1)
                        dve.tensor_tensor(exm[h][:, :, CH:2 * CH], e1[:], exm[h][:, :, 0:CH], ALU.mult)
                        dve.drain().then_inc(s_p, 1)
                    dve.reg_add(step, step, 1)
                g = dve.snap(step, min_val=1, max_val=MANY)
                accumulate(1, g * 2 + 2)
                for h in range(2):
                    tile = bass.ds(q * 2 + h, 1)
                    dve.reciprocal(rden[:], acc[h][:, 0, :])
                    dve.drain()
                    dve.tensor_tensor(ratio[:], acc[h][:, 1, :], rden[:], ALU.mult)
                    dve.drain()
                    dve.tensor_reduce(ft_p[:, tile, :].rearrange("p a f -> p (a f)"),
                                      ratio[:].rearrange("p (i o) -> p o i", o=FEAT), AX_X, ALU.add)
                    dve.drain()
            dve.drain().then_inc(s_ft, 1)
            dve.wait_ge(s_ftn, 16)
            dve.tensor_tensor(x2[:], x2[:], has_edge[:].unsqueeze(2).broadcast_to(wide), ALU.mult)
            dve.drain()
            dve.tensor_tensor(x2[:], x2[:], x1[:], ALU.add)
            layernorm(x2, x2_sq[:], 2)
            dve.drain().then_inc(s_x2, 1)


_INS = ['x', 'src', 'dst', 'edge_attr_16', 'L0_gnn_W1', 'L0_gnn_b1', 'L0_gnn_W2', 'L0_gnn_b2', 'L0_gnn_W3',
        'L0_gnn_b3', 'L1_gnn_W_msg', 'L1_gnn_b_msg', 'L1_gnn_W_attn', 'L1_gnn_b_attn']
_PADDED = {'x': (NP, 0), 'src': (EP, 0), 'dst': (EP, FAR), 'edge_attr_16': (E + SLOT, 0)}


def kernel(**inputs):
    import numpy as _np
    import concourse.bacc as _bacc
    from concourse import mybir as _mybir
    from concourse.bass_utils import run_bass_kernel_spmd as _run

    nc = _bacc.Bacc("TRN2", target_bir_lowering=False, num_devices=1)
    arrays, args = {}, []
    for name in _INS:
        a = _np.ascontiguousarray(inputs[name])
        if name in _PADDED:
            rows, value = _PADDED[name]
            full = _np.full((rows,) + a.shape[1:], value, a.dtype)
            full[:a.shape[0]] = a
            a = full
        arrays[f"in_{name}_dram"] = a
        args.append(nc.dram_tensor(f"in_{name}_dram", a.shape, _mybir.dt.from_np(a.dtype), kind="ExternalInput").ap())
    args.append(nc.dram_tensor("out_0_dram", (N, FEAT), F32, kind="ExternalOutput").ap())
    gnn_kernel(nc, *args)
    r = _run(nc, [arrays], core_ids=[0])
    return r.results[0]["out_0_dram"]
```
